# Optimizing a Trainium2 kernel written in Bass

```python
import numpy as np
import jax
import jax.numpy as jnp

def _softmax(x, axis=-1):
    return jax.nn.softmax(x, axis=axis)

def _gelu(x):
    return jax.nn.gelu(x, approximate=True)

def _silu(x):
    return jax.nn.silu(x)

def _sigmoid(x):
    return jax.nn.sigmoid(x)

def _layernorm(x, axis=-1, eps=1e-05):
    m = jnp.mean(x, axis=axis, keepdims=True)
    v = jnp.var(x, axis=axis, keepdims=True)
    return (x - m) / jnp.sqrt(v + eps)

def _scatter_add(tgt, idx, src, axis=0):
    return tgt.at[idx].add(src)

def _segment_sum(src, seg, n):
    return jax.ops.segment_sum(src, seg, n)
kernel_name = 'mk_adj_preln_d1_adj_r2_9be7b9'

def setup_inputs(seed: int=0):
    np.random.seed(seed)
    _w = jnp.asarray

    def _rec_inputs():
        import jax
        import jax.numpy as jnp
        _gk = jax.random.key(seed)
        x = -0.0002928 + 1 * jax.random.normal(jax.random.fold_in(_gk, 1), (8192, 256), jnp.float32)
        _a = jax.random.bernoulli(jax.random.fold_in(_gk, 2), 0.000244141, (8192, 8192))
        _a = jnp.logical_or(_a, jnp.swapaxes(_a, -1, -2))
        _a = jnp.logical_or(_a, jnp.eye(8192, dtype=bool))
        adj = _a.astype(jnp.int32)
        return (x, adj)
    x, adj = _rec_inputs()

    def _L0_gnn_setup():
        import jax, jax.numpy as jnp
        import numpy as np
        N = 4096
        IN_F = 256
        OUT_F = 256
        ALPHA = 0.2
        key = jax.random.key(seed)
        k1, k2, k3, k4, k5 = jax.random.split(key, 5)
        inp = jax.random.normal(k1, (N, IN_F), dtype=jnp.float32)
        adj = jax.random.randint(k2, (N, N), 0, 2, dtype=jnp.int32)
        W1 = jax.random.normal(k3, (IN_F, OUT_F), dtype=jnp.float32) * (1.0 / np.sqrt(IN_F))
        b1 = jnp.zeros((OUT_F,), dtype=jnp.float32)
        a = jax.random.normal(k4, (2 * OUT_F,), dtype=jnp.float32) * (1.0 / np.sqrt(2 * OUT_F))
        a1 = a[:OUT_F]
        a2 = a[OUT_F:]
        b2 = jnp.zeros((), dtype=jnp.float32)
        return {'inp': inp, 'adj': adj, 'W1': W1, 'b1': b1, 'a1': a1, 'a2': a2, 'b2': b2}
    _L0_gnn_all = _L0_gnn_setup()
    _L0_gnn_in = {k: v for k, v in _L0_gnn_all.items() if k in ('W1', 'b1', 'a1', 'a2', 'b2')}
    del _L0_gnn_all
    return {'x': x, 'adj': adj, 'L0_gnn_W1': _L0_gnn_in['W1'], 'L0_gnn_b1': _L0_gnn_in['b1'], 'L0_gnn_a1': _L0_gnn_in['a1'], 'L0_gnn_a2': _L0_gnn_in['a2'], 'L0_gnn_b2': _L0_gnn_in['b2']}

def reference(x, adj, L0_gnn_W1, L0_gnn_b1, L0_gnn_a1, L0_gnn_a2, L0_gnn_b2):
    import jax
    import jax.numpy as jnp

    def _L0_gnn_ref(inp, adj, W1, b1, a1, a2, b2):
        import jax, jax.numpy as jnp
        import numpy as np
        N = 4096
        IN_F = 256
        OUT_F = 256
        ALPHA = 0.2
        h = inp @ W1 + b1
        e = jax.nn.leaky_relu((h @ a1)[:, None] + (h @ a2)[None, :] + b2, ALPHA)
        attention = jnp.where(adj > 0, e, jnp.float32(-1000000000000.0))
        attention = jax.nn.softmax(attention, axis=1)
        h_prime = attention @ h
        return jax.nn.elu(h_prime)
    h = jnp.maximum(_layernorm(x, axis=-1), 0.0)
    x = x + _L0_gnn_ref(h, adj, L0_gnn_W1, L0_gnn_b1, L0_gnn_a1, L0_gnn_a2, L0_gnn_b2)
    return x

_drawn_inputs = setup_inputs


def setup_inputs(seed=0):
    import zlib

    import numpy as np

    out = dict(_drawn_inputs(seed))
    spreads = {'L0_gnn_b1': (0.0, 0.1)}
    factors = {'L0_gnn_a1': 2.805}
    for name, (base, spread) in spreads.items():
        noise = np.random.default_rng([zlib.crc32(name.encode()), seed]).standard_normal(out[name].shape)
        drawn = base * np.exp(spread * noise) if base else spread * noise
        out[name] = jnp.asarray(drawn.astype(out[name].dtype))
    for name, factor in factors.items():
        out[name] = (out[name] * factor).astype(out[name].dtype)
    return out
```

```python
import numpy as np
import concourse.bass as bass
from concourse import mybir
from contextlib import ExitStack

F32, BF16, I32, I16 = mybir.dt.float32, mybir.dt.bfloat16, mybir.dt.int32, mybir.dt.int16
ALU = mybir.AluOpType
ACT = mybir.ActivationFunctionType
AX = mybir.AxisListType.X
RMAX = bass.bass_isa.ReduceOp.max

P = 128
N, D = 8192, 256
KD = D // P
BITS = 8
PACK_ROWS = P * BITS
PACKS = N // PACK_ROWS
TILES = N // P
TPP = TILES // PACKS
STEP_COLS = N // TPP
SUB = 512
SEGS = 8
SLOTS = P // 2
PAIRS = TPP
GROUP_COLS = 2
WORD = 2 << BITS
EMPTY = (1 << BITS) - 1
LOWEST = 0.5 - EMPTY
S2, ONE = D, D + 1
S1 = D + 1
ROW = D + 1
WIDE = D + 2
ALPHA = 0.2
EPS = 1e-5
MASKED = -1000000000000.0
SPREAD = 60.0
BATCH = 4
BATCHES = TILES // BATCH
JB = 8


class Order:

    def __init__(self, eng, sem, passed, start=0):
        self.eng, self.sem, self.passed, self.n = eng, sem, passed, start

    def link(self, instruction, apart=False):
        instruction.then_inc(self.sem, 1)
        self.n = self.n + 1
        if apart:
            wait_apart(self.eng, self.sem, self.n, self.passed)
        else:
            self.eng.wait_ge(self.sem, self.n)


def wait_apart(eng, sem, value, passed):
    eng.wait_ge(sem, value)
    eng.sem_inc(passed, 1)


def gat_kernel(nc, x, adj, W1, b1, a1, a2, b2, out):
    ctx = ExitStack()
    with ctx:
        def sb(name, shape, dt=F32):
            return ctx.enter_context(nc.sbuf_tensor(name, shape, dt))

        def sem(name):
            return ctx.enter_context(nc.semaphore(name))

        table = nc.dram_tensor("table", (N, ROW), F32, kind="Internal").ap()
        s2_dram = nc.dram_tensor("s2_dram", (TILES, P), F32, kind="Internal").ap()

        adj_sb = sb("adj_sb", [P, 4, BITS, SUB], I32)
        signs = sb("signs", [P, 2, BITS, SUB], BF16)
        gathered = sb("gathered", [P, 2, PAIRS, WIDE])
        s1_max = sb("s1_max", [P, 2, TILES, SLOTS])
        column = sb("column", [P, N], I16)
        key = sb("key", [P, 2, STEP_COLS])
        weights = sb("weights", [P, 2, PAIRS, P])
        row_bit = sb("row_bit", [P, SLOTS, BITS], I32)
        bit_mask = sb("bit_mask", [P, BITS], I32)
        top8 = sb("top8", [P, 2, SEGS, 8])
        winners = sb("winners", [P, TPP, SEGS * 8])
        slots = sb("slots", [P, SLOTS])
        slots_twice = sb("slots_twice", [P, 2, SLOTS])
        words = sb("words", [P, SLOTS], I32)
        words_less = sb("words_less", [P, SLOTS], I32)
        index = sb("index", [P, SLOTS], I32)
        index_now = sb("index_now", [P, 2, PAIRS], I32)
        logits = sb("logits", [P, 2, PAIRS * BITS])
        exps = sb("exps", [P, 2, PAIRS * BITS])
        relu_out = sb("relu_out", [P, 2, D])
        exp_out = sb("exp_out", [P, 2, D])
        x_again = sb("x_again", [P, 2, D])
        result = sb("result", [P, 2, D])
        recip = sb("recip", [P, 2])
        density = sb("density", [P, TILES])
        full = sb("full", [P, 2, PACKS])
        x_in = sb("x_in", [P, 2, BATCH, D])
        normed = sb("normed", [P, BATCH, D])
        acts_t = sb("acts_t", [P, KD, BATCH * P])
        stats = sb("stats", [P, BATCH, 6])
        mean_var = sb("mean_var", [P, BATCH, 2])
        std = sb("std", [P, BATCH])
        rstd = sb("rstd", [P, BATCH])
        w_ext = sb("w_ext", [P, KD, WIDE])
        bias_ext = sb("bias_ext", [P, WIDE])
        a_rows = sb("a_rows", [P, 2, D])
        b2_col = sb("b2_col", [P, 1])
        product = sb("product", [P, D])
        u1_rep = sb("u1_rep", [P, KD, P])
        s_cols = sb("s_cols", [P, TILES, 2])
        ident = sb("ident", [P, P])
        ident_bf = sb("ident_bf", [P, P], BF16)
        scaled = sb("scaled", [P, BITS, P], BF16)
        eps_col = sb("eps_col", [P, 1])
        below = sb("below", [P, 1])
        zero_col = sb("zero_col", [P, 1])
        extremes = sb("extremes", [P, 2])
        bounds = sb("bounds", [P, 2])
        checks = sb("checks", [P, 8])
        flag_f = sb("flag_f", [P, 1])
        flag = sb("flag", [P, 1], I32)

        ps = ctx.enter_context(nc.psum_tensor("ps", [P, 8, SUB], F32))
        turned = ps[:, 0:2, :].rearrange("p k c -> p (k c)")
        h_ps = ps[:, 2:2 + BATCH, 0:WIDE]
        s1_ps = ps[:, 6, :]
        sums = [ps[:, 2 * q:2 * q + 2, :].rearrange("p k c -> p (k c)") for q in range(2)]
        slots_ps = ps[:, 6, 0:P]
        out_ps = [ps[:, 4 + q, 0:WIDE] for q in range(2)]

        adj_in = [sem(f"adj_in{i}") for i in range(4)]
        signs_done = sem("signs_done")
        packs_done = sem("packs_done")
        sums_read = sem("sums_read")
        winners_kept = sem("winners_kept")
        slots_ready = sem("slots_ready")
        slots_turned = sem("slots_turned")
        index_ready = sem("index_ready")
        index_copied = sem("index_copied")
        rows_in = [sem(f"rows_in{i}") for i in range(2)]
        logits_ready = sem("logits_ready")
        exps_ready = sem("exps_ready")
        weights_ready = sem("weights_ready")
        pv_done = sem("pv_done")
        recip_ready = sem("recip_ready")
        acts_done = sem("acts_done")
        x_again_in = [sem(f"x_again_in{i}") for i in range(2)]
        result_ready = sem("result_ready")
        out_stored = [sem(f"out_stored{i}") for i in range(2)]
        list_order = sem("list_order")
        pack_order = sem("pack_order")
        attend_order = sem("attend_order")
        x_in_sem = [sem(f"x_in{i}") for i in range(2)]
        params_in = sem("params_in")
        ident_ready = sem("ident_ready")
        pool_consts = sem("pool_consts")
        scaled_ready = sem("scaled_ready")
        setup_order = sem("setup_order")
        proj_order = sem("proj_order")
        var_ready = sem("var_ready")
        std_ready = sem("std_ready")
        normed_ready = sem("normed_ready")
        turned_ready = sem("turned_ready")
        acts_t_ready = sem("acts_t_ready")
        h_ready = sem("h_ready")
        h_read = sem("h_read")
        table_stored = [sem(f"table_stored{i}") for i in range(2)]
        extremes_ready = sem("extremes_ready")
        bounds_ready = sem("bounds_ready")
        attend_ready = sem("attend_ready")
        checks_ready = sem("checks_ready")
        checks_done = sem("checks_done")
        flag_ready = sem("flag_ready")
        passed = sem("passed")
        g_turn = sem("g_turn")
        g_s2 = sem("g_s2")
        g_s2_stored = sem("g_s2_stored")
        g_s2_in = sem("g_s2_in")
        g_order = sem("g_order")
        g_row_in = sem("g_row_in")
        g_scores = sem("g_scores")
        g_exps = sem("g_exps")
        g_h_in = sem("g_h_in")
        g_block = sem("g_block")
        g_block_ps = sem("g_block_ps")
        g_block_t = sem("g_block_t")
        g_part = sem("g_part")
        g_added = sem("g_added")
        g_low = sem("g_low")
        g_exp_out = sem("g_exp_out")
        g_result = sem("g_result")
        g_stored = sem("g_stored")

        adj_v = adj.rearrange("(b g t) (o s c) -> b o s g t c", g=P, t=BITS, s=2, c=SUB)
        x_batch = x.rearrange("(m i p) f -> m p i f", i=BATCH, p=P)
        table_batch = table.rearrange("(m i p) f -> m p i f", i=BATCH, p=P)
        x_tile = x.rearrange("(k p) f -> k p f", p=P)
        out_tile = out.rearrange("(k p) f -> k p f", p=P)

        h_sb = [gathered[:, q, 0:BATCH, :] for q in range(2)]
        s1_half = s1_max[:, 0, :, :]
        m_half = s1_max[:, 1, :, :]

        flat = adj_sb[:, :, :, :].rearrange("p a t c -> p (a t c)")
        g_row, g_rowf = flat[:, 0:N], flat[:, 0:N].bitcast(F32)
        g_e = flat[:, N:2 * N].bitcast(F32)
        g_s2b = s1_max[:, :, :, :].rearrange("p a t c -> p (a t c)")
        g_h = gathered[:, :, :, :].rearrange("p a t c -> p (a t c)")[:, 0:JB * D].rearrange("p (j f) -> p j f", j=JB)
        g_blk, g_blk_t = weights[:, 0, 0, :], weights[:, 0, 1, :]
        g_acc = weights[:, 1, 0:2, :].rearrange("p a c -> p (a c)")
        table_jb = table.rearrange("(b j p) f -> b p j f", j=JB, p=P)

        block = ctx.enter_context(nc.Block())

        def general_loads(sp):
            sp.wait_ge(g_s2, 1)
            sp.dma_start(s2_dram, product[0:TILES, 0:P]).then_inc(g_s2_stored, 16)
            sp.wait_ge(g_s2_stored, 16)
            sp.dma_start(g_s2b, s2_dram.rearrange("(o i) p -> o (i p)", o=1).broadcast_to([P, N])).then_inc(g_s2_in, 16)
            with sp.Fori(0, TILES) as i:
                wait_apart(sp, g_scores, i + 1, passed)
                wait_apart(sp, g_stored, 16 * i + 16, passed)
                sp.dma_start(g_row, adj.rearrange("(i p) n -> i p n", p=P)[i]).then_inc(g_row_in, 16)
                sp.dma_start(x_again[:, 0, :], x_tile[i]).then_inc(g_row_in, 16)
                with sp.Fori(0, TILES // JB) as jb:
                    wait_apart(sp, g_part, i * TILES + jb * JB + 1, passed)
                    sp.dma_start(g_h, table_jb[jb][:, :, 0:D]).then_inc(g_h_in, 16)
                wait_apart(sp, g_result, i + 1, passed)
                sp.dma_start(out_tile[i], result[:, 0, :]).then_inc(g_stored, 16)
            wait_apart(sp, g_stored, 16 * TILES + 16, passed)

        def general_scalar(act):
            with act.Fori(0, TILES) as i:
                act.wait_ge(g_scores, i + 2)
                nc.scalar.activation(g_e, g_e, ACT.Exp, bias=checks[:, 1:2], accum_out=checks[:, 2:3]).then_inc(g_exps, 1)
                act.wait_ge(g_low, i + 1)
                nc.scalar.activation(exp_out[:, 0, :], exp_out[:, 0, :], ACT.Exp, bias=zero_col[:, :]).then_inc(g_exp_out, 1)

        def general_tensor(pe):
            nc.tensor.transpose(ps[0:TILES, 0, 0:P], s_cols[:, :, 0], ident[:, :]).then_inc(g_turn, 1)
            with pe.Fori(0, TILES) as i:
                with pe.Fori(0, TILES // JB) as jb:
                    for jj in range(JB):
                        u = i * TILES + jb * JB + jj
                        pe.wait_ge(g_block, u + 1)
                        nc.tensor.transpose(ps[:, 1, 0:P], g_blk, ident[:, :]).then_inc(g_block_ps, 1)
                        pe.wait_ge(g_block_t, u + 1)
                        pe.wait_ge(g_h_in, 16 * (i * (TILES // JB) + jb + 1))
                        nc.tensor.matmul(ps[:, 2, 0:D], g_blk_t, g_h[:, jj, :], start=True, stop=True).then_inc(g_part, 1)

        def general_vector(dve):
            dve.sem_inc(g_scores, 1)
            dve.sem_inc(g_stored, 16)
            dve.sem_inc(g_part, 1)
            dve.wait_ge(g_turn, 1)
            nc.vector.tensor_copy(product[0:TILES, 0:P], ps[0:TILES, 0, 0:P]).then_inc(g_s2, 1)
            dve.wait_ge(g_s2_in, 16)
            with dve.Fori(0, TILES) as i:
                order = Order(dve, g_order, passed, i * GENERAL_LINKS)
                dve.wait_ge(g_row_in, 32 * i + 32)
                dve.wait_ge(g_part, i * TILES + 1)
                order.link(nc.vector.tensor_copy(checks[:, 0:1], s_cols[:, bass.ds(i, 1), 1]))
                order.link(nc.vector.tensor_scalar(g_e, g_s2b, checks[:, 0:1], None, ALU.add))
                order.link(nc.vector.scalar_tensor_tensor(g_e, g_e, ALPHA, g_e, ALU.mult, ALU.max))
                order.link(nc.vector.scalar_tensor_tensor(g_e, g_row, 0.0, g_e, ALU.is_gt, ALU.mult))
                order.link(nc.vector.tensor_scalar(g_rowf, g_row, 0.0, MASKED, ALU.is_le, ALU.mult))
                order.link(nc.vector.tensor_tensor(g_e, g_e, g_rowf, ALU.add))
                order.link(nc.vector.reduce_max(checks[:, 3:4], g_e, AX))
                order.link(nc.vector.memset(g_acc, 0.0))
                nc.vector.tensor_scalar(checks[:, 1:2], checks[:, 3:4], -1.0, None, ALU.mult).then_inc(g_scores, 1)
                wait_apart(dve, g_exps, i + 1, passed)
                order.link(nc.vector.reciprocal(checks[:, 4:5], checks[:, 2:3]), apart=True)
                with dve.Fori(0, TILES // JB) as jb:
                    for jj in range(JB):
                        u = i * TILES + jb * JB + jj
                        nc.vector.tensor_copy(g_blk, g_e[:, bass.ds((jb * JB + jj) * P, P)]).then_inc(g_block, 1)
                        dve.wait_ge(g_block_ps, u + 1)
                        nc.vector.tensor_copy(g_blk_t, ps[:, 1, 0:P]).then_inc(g_block_t, 1)
                        dve.wait_ge(g_part, u + 2)
                        nc.vector.tensor_tensor(g_acc, g_acc, ps[:, 2, 0:D], ALU.add).then_inc(g_added, 1)
                        dve.wait_ge(g_added, u + 1)
                dve.wait_ge(g_stored, 16 * i + 16)
                order.link(nc.vector.tensor_scalar(relu_out[:, 0, :], g_acc, checks[:, 4:5], 0.0, ALU.mult, ALU.max))
                nc.vector.tensor_scalar(exp_out[:, 0, :], g_acc, checks[:, 4:5], 0.0, ALU.mult, ALU.min).then_inc(g_low, 1)
                dve.wait_ge(g_exp_out, i + 1)
                order.link(nc.vector.scalar_tensor_tensor(exp_out[:, 0, :], exp_out[:, 0, :], -1.0, relu_out[:, 0, :],
                                                          ALU.add, ALU.add))
                nc.vector.tensor_tensor(result[:, 0, :], exp_out[:, 0, :], x_again[:, 0, :], ALU.add).then_inc(g_result, 1)

        @block.sync
        def _(sp):
            def load_adj(b, j, wait=True):
                for p in range(2):
                    for s in range(2):
                        i = 2 * p + s
                        if wait:
                            wait_apart(sp, signs_done, 16 * b + 4 * j + i + 1, passed)
                        sp.dma_start(adj_sb[:, i, :, :], adj_v[b, 2 * j + p, s]).then_inc(adj_in[i], 16)

            sp.dma_start(w_ext[:, :, 0:D], W1.rearrange("(k p) f -> p k f", p=P)).then_inc(params_in, 16)
            sp.dma_start(a_rows[:, 0, :], a1.rearrange("(o f) -> o f", o=1).broadcast_to([P, D])).then_inc(params_in, 16)
            sp.dma_start(a_rows[:, 1, :], a2.rearrange("(o f) -> o f", o=1).broadcast_to([P, D])).then_inc(params_in, 16)
            sp.dma_start(bias_ext[:, 0:D], b1.rearrange("(o f) -> o f", o=1).broadcast_to([P, D])).then_inc(params_in, 16)
            sp.dma_start(b2_col[:, :], b2.broadcast_to([P, 1])).then_inc(params_in, 16)
            for q in range(2):
                sp.dma_start(x_in[:, q, :, :], x_batch[q]).then_inc(x_in_sem[q], 16)
            load_adj(0, 0, wait=False)
            def store_rows(m, q):
                wait_apart(sp, h_read, 2 * m + q + 2, passed)
                sp.dma_start(table_batch[2 * m + q], h_sb[q][:, :, 0:ROW]).then_inc(table_stored[q], 16)

            with sp.Fori(0, BATCHES // 2 - 1) as m:
                for q in range(2):
                    store_rows(m, q)
                    sp.dma_start(x_in[:, q, :, :], x_batch[2 * m + 2 + q]).then_inc(x_in_sem[q], 16)
            for q in range(2):
                store_rows(BATCHES // 2 - 1, q)
            with sp.Fori(1, TPP // 2) as j:
                load_adj(0, j)
            with sp.Fori(1, PACKS) as b:
                with sp.Fori(0, TPP // 2) as j:
                    load_adj(b, j)
            sp.wait_ge(flag_ready, 1)
            needed = sp.value_load(flag[0:1, 0:1], min_val=0, max_val=1)
            with sp.If(needed != 0):
                general_loads(sp)
            sp.nop()

        @block.gpsimd
        def _(pool):
            pool.memset(ident[:, :], 0.0).then_inc(ident_ready, 1)
            pool.iota(column[:, :], pattern=[[1, N]], base=0, channel_multiplier=0).then_inc(pool_consts, 1)
            pool.wait_ge(ident_ready, 1)
            pool.affine_select(out=ident[:, :], in_=ident[:, :], compare_op=ALU.not_equal, fill=1.0, base=0,
                               pattern=[[-1, P]], channel_multiplier=1).then_inc(ident_ready, 1)
            pool.wait_ge(extremes_ready, 1)
            pool.partition_all_reduce(bounds[:, :], extremes[:, :], P, RMAX).then_inc(bounds_ready, 1)
            for q in range(2):
                pool.wait_ge(table_stored[q], 16 * (BATCHES // 2) + 16)
            pool.wait_ge(attend_ready, 1)

            with pool.Fori(0, PACKS) as b:
                wait_apart(pool, index_ready, b + 1, passed)
                with pool.Fori(0, TPP // 2) as j:
                    for p in range(2):
                        k = b * TPP + 2 * j + p
                        pool.wait_ge(pv_done, k + 1)
                        pool.tensor_copy(index_now[:, p, :], index[:, bass.ds((2 * j + p) * PAIRS, PAIRS)])\
                            .then_inc(index_copied, 1)
                        wait_apart(pool, index_copied, k + 1, passed)
                        for q in range(PAIRS):
                            pool.indirect_dma_start(
                                out=gathered[:, p, q, 0:ROW], out_offset=None, in_=table,
                                in_offset=bass.IndirectOffsetOnAxis(ap=index_now[:, p, q:q + 1], axis=0),
                                bounds_check=N - 1, oob_is_err=False).then_inc(rows_in[p], 16)
            pool.wait_ge(checks_ready, 1)
            pool.partition_all_reduce(flag_f[:, :], checks[:, 0:1], P, RMAX).then_inc(checks_done, 1)
            pool.wait_ge(checks_done, 1)
            pool.tensor_copy(flag[:, :], flag_f[:, :]).then_inc(flag_ready, 1)

        @block.scalar
        def _(act):
            act.sem_inc(acts_done, 2)
            act.sem_inc(signs_done, 4)
            with act.Fori(0, BATCHES) as m:
                act.wait_ge(var_ready, m + 1)
                nc.scalar.activation(std[:, :], mean_var[:, :, 1], ACT.Sqrt, bias=eps_col[:, :]).then_inc(std_ready, 1)
                act.wait_ge(turned_ready, m + 2)
                for k in range(KD):
                    last = nc.scalar.activation(acts_t[:, k, :], turned[:, k * BATCH * P:(k + 1) * BATCH * P], ACT.Relu)
                last.then_inc(acts_t_ready, 1)

            def take_signs(b, j, p, s):
                i = 2 * p + s
                n = 16 * b + 4 * j + i
                act.wait_ge(adj_in[i], 64 * b + 16 * j + 16)
                act.wait_ge(packs_done, n + 1)
                nc.scalar.activation(signs[:, s, :, :], adj_sb[:, i, :, :], ACT.Sign,
                                     bias=below[:, :]).then_inc(signs_done, 1)

            def fetch_x(k, p):
                act.wait_ge(result_ready, k + 1)
                act.dma_start(x_again[:, p, :], x_tile[k]).then_inc(x_again_in[p], 16)

            def exponents(k, p):
                act.wait_ge(logits_ready, k + 1)
                nc.scalar.activation(exps[:, p, :], logits[:, p, :], ACT.Exp, bias=zero_col[:, :]).then_inc(exps_ready, 1)

            def normalise(k, p):
                act.wait_ge(recip_ready, k + 1)
                nc.scalar.activation(relu_out[:, p, :], out_ps[p][:, 0:D], ACT.Relu, scale=recip[:, p:p + 1])
                nc.scalar.activation(exp_out[:, p, :], out_ps[p][:, 0:D], ACT.Exp, bias=zero_col[:, :],
                                     scale=recip[:, p:p + 1]).then_inc(acts_done, 1)

            def store(k, p):
                act.wait_ge(result_ready, k + 3)
                act.dma_start(out_tile[k], result[:, p, :]).then_inc(out_stored[p], 16)

            with act.Fori(0, TPP // 2) as j:
                for p in range(2):
                    for s in range(2):
                        take_signs(0, j, p, s)
            with act.Fori(1, PACKS) as b:
                with act.Fori(0, TPP // 2) as j:
                    for p in range(2):
                        k = (b - 1) * TPP + 2 * j + p
                        fetch_x(k, p)
                        take_signs(b, j, p, 0)
                        exponents(k, p)
                        take_signs(b, j, p, 1)
                        normalise(k, p)
                        store(k, p)
            with act.Fori(0, TPP // 2) as j:
                for p in range(2):
                    k = (PACKS - 1) * TPP + 2 * j + p
                    fetch_x(k, p)
                    exponents(k, p)
                    normalise(k, p)
                    store(k, p)
            for p in range(2):
                act.wait_ge(out_stored[p], 16 * (TILES // 2) + 16)
            act.wait_ge(flag_ready, 1)
            needed = act.value_load(flag[0:1, 0:1], min_val=0, max_val=1)
            with act.If(needed != 0):
                general_scalar(act)
            act.nop()

        @block.tensor
        def _(pe):
            pe.sem_inc(turned_ready, 1)
            pe.sem_inc(packs_done, 2)
            pe.sem_inc(pv_done, 2)
            pe.wait_ge(ident_ready, 2)
            with pe.Fori(0, BATCHES) as m:
                pe.wait_ge(normed_ready, m + 1)
                for k in range(KD):
                    for i in range(BATCH):
                        last = nc.tensor.transpose(turned[:, (k * BATCH + i) * P:(k * BATCH + i + 1) * P],
                                                   normed[:, i, k * P:(k + 1) * P], ident[:, :])
                last.then_inc(turned_ready, 1)
                pe.wait_ge(acts_t_ready, m + 1)
                pe.wait_ge(h_read, m + 1)
                for k in range(KD):
                    nc.tensor.matmul(s1_ps, u1_rep[:, k, :], acts_t[:, k, :], start=(k == 0), stop=(k == KD - 1))
                for i in range(BATCH):
                    for k in range(KD):
                        last = nc.tensor.matmul(h_ps[:, i, :], acts_t[:, k, i * P:(i + 1) * P], w_ext[:, k, :],
                                                start=(k == 0), stop=(k == KD - 1))
                last.then_inc(h_ready, 1)

            def add_signs(b, j, p):
                k = TPP * b + 2 * j + p
                pe.wait_ge(sums_read, k + 1)
                for s in range(2):
                    pe.wait_ge(signs_done, 2 * k + s + 5)
                    for t in range(BITS):
                        last = nc.tensor.matmul(sums[p][:, s * SUB:(s + 1) * SUB], scaled[:, t, :], signs[:, s, t, :],
                                                start=(t == 0), stop=(t == BITS - 1))
                    last.then_inc(packs_done, 1)

            def turn_slots(b):
                pe.wait_ge(slots_ready, b + 1)
                nc.tensor.transpose(slots_ps, slots_twice[:, :, :].rearrange("p a c -> p (a c)"), ident[:, :])\
                    .then_inc(slots_turned, 1)

            def weigh(k, p):
                pe.wait_ge(weights_ready, 2 * k + 2)
                pe.wait_ge(acts_done, k + 1)
                for q in range(PAIRS):
                    last = nc.tensor.matmul(out_ps[p], weights[:, p, q, :], gathered[:, p, q, :],
                                            start=(q == 0), stop=(q == PAIRS - 1))
                last.then_inc(pv_done, 1)

            pe.wait_ge(scaled_ready, BITS)
            pe.wait_ge(h_read, BATCHES + 1)
            with pe.Fori(0, TPP // 2) as j:
                for p in range(2):
                    add_signs(0, j, p)
            turn_slots(0)
            with pe.Fori(1, PACKS) as b:
                with pe.Fori(0, TPP // 2) as j:
                    for p in range(2):
                        add_signs(b, j, p)
                        weigh((b - 1) * TPP + 2 * j + p, p)
                turn_slots(b)
            with pe.Fori(0, TPP // 2) as j:
                for p in range(2):
                    weigh((PACKS - 1) * TPP + 2 * j + p, p)
            pe.wait_ge(flag_ready, 1)
            needed = pe.value_load(flag[0:1, 0:1], min_val=0, max_val=1)
            with pe.If(needed != 0):
                general_tensor(pe)
            pe.nop()

        @block.vector
        def _(dve):
            dve.sem_inc(h_read, 1)
            for q in range(2):
                dve.sem_inc(table_stored[q], 16)
                dve.sem_inc(out_stored[q], 16)
            dve.sem_inc(sums_read, 2)
            dve.sem_inc(result_ready, 2)
            nc.vector.memset(eps_col[:, :], EPS)
            nc.vector.memset(below[:, :], -0.5)
            nc.vector.memset(zero_col[:, :], 0.0)
            nc.vector.memset(weights[:, :, :, :], 0.0)
            for t in range(BITS):
                nc.vector.memset(bit_mask[:, t:t + 1], 2 << t)
            dve.wait_ge(params_in, 80)
            setup = Order(dve, setup_order, passed)
            for c, a in ((S2, 1), (S1, 0)):
                for k in range(KD):
                    setup.link(nc.vector.tensor_tensor(product[:, :], w_ext[:, k, 0:D], a_rows[:, a, :], ALU.mult))
                    setup.link(nc.vector.reduce_sum(w_ext[:, k, c:c + 1], product[:, :], AX))
                setup.link(nc.vector.tensor_tensor(product[:, :], bias_ext[:, 0:D], a_rows[:, a, :], ALU.mult))
                setup.link(nc.vector.reduce_sum(bias_ext[:, c:c + 1], product[:, :], AX))
            setup.link(nc.vector.tensor_tensor(bias_ext[:, S1:S1 + 1], bias_ext[:, S1:S1 + 1], b2_col[:, :], ALU.add))
            for k in range(KD):
                setup.link(nc.vector.tensor_copy(u1_rep[:, k, :], w_ext[:, k, S1:S1 + 1].broadcast_to([P, P])))
            dve.wait_ge(ident_ready, 2)
            for t in range(BITS):
                nc.vector.tensor_scalar(scaled[:, t, :], ident[:, :], float(1 << t), None, ALU.mult)\
                    .then_inc(scaled_ready, 1)

            with dve.Fori(0, BATCHES // 2) as half:
                for q in range(2):
                    m = 2 * half + q
                    proj = Order(dve, proj_order, passed, m * PROJ_LINKS)
                    dve.wait_ge(x_in_sem[q], 16 * half + 16)
                    for i in range(BATCH):
                        last = nc.vector.bn_stats(stats[:, i, :], x_in[:, q, i, :])
                    proj.link(last, apart=True)
                    for i in range(BATCH):
                        last = nc.vector.bn_aggr(mean_var[:, i, :], stats[:, i, :])
                    last.then_inc(var_ready, 1)
                    dve.wait_ge(std_ready, m + 1)
                    proj.link(nc.vector.reciprocal(rstd[:, :], std[:, :]))
                    dve.wait_ge(turned_ready, m + 1)
                    for i in range(BATCH):
                        last = nc.vector.tensor_scalar(normed[:, i, :], x_in[:, q, i, :], mean_var[:, i, 0:1],
                                                       rstd[:, i:i + 1], ALU.subtract, ALU.mult)
                    last.then_inc(normed_ready, 1)
                    dve.wait_ge(h_ready, m + 1)
                    dve.wait_ge(table_stored[q], 16 * half + 16)
                    proj.link(nc.vector.tensor_tensor(
                        h_sb[q], h_ps, bias_ext[:, :].rearrange("p (o f) -> p o f", o=1).broadcast_to([P, BATCH, WIDE]), ALU.add))
                    nc.vector.tensor_copy(s_cols[:, bass.ds(m * BATCH, BATCH), :], h_sb[q][:, :, S2:S2 + 2])
                    for g in range(GROUP_COLS):
                        rows = slice(g * SLOTS, (g + 1) * SLOTS)
                        last = nc.vector.tensor_scalar(
                            s1_half[rows, bass.ds(m * BATCH, BATCH), :].rearrange("p i (q t) -> p (i q) t", t=BITS),
                            s1_ps[rows, :].rearrange("p (n g t) -> p n g t", g=GROUP_COLS, t=BITS)[:, :, g, :],
                            bias_ext[rows, S1:S1 + 1], None, ALU.add)
                    last.then_inc(h_read, 1)

            dve.wait_ge(h_read, BATCHES + 1)
            setup.link(nc.vector.reduce_max(extremes[:, 0:1], s_cols[:, :, 0], AX))
            setup.link(nc.vector.tensor_reduce(checks[:, 1:2], s_cols[:, :, 0], AX, ALU.min))
            nc.vector.tensor_scalar(extremes[:, 1:2], checks[:, 1:2], -1.0, None, ALU.mult).then_inc(extremes_ready, 1)
            dve.wait_ge(bounds_ready, 1)
            flat_s1 = s1_half.rearrange("p i c -> p (i c)")
            flat_m = m_half.rearrange("p i c -> p (i c)")
            setup.link(nc.vector.tensor_scalar(flat_m, flat_s1, bounds[:, 0:1], None, ALU.add))
            setup.link(nc.vector.scalar_tensor_tensor(flat_m, flat_m, ALPHA, flat_m, ALU.mult, ALU.max))
            for q in range(2):
                dve.wait_ge(table_stored[q], 16 * (BATCHES // 2) + 16)
            setup.link(nc.vector.memset(gathered[:, :, :, 0:D], 0.0))
            setup.link(nc.vector.memset(gathered[:, :, :, S2:S2 + 1], -1e30))
            nc.vector.memset(gathered[:, :, :, ONE:ONE + 1], 1.0).then_inc(attend_ready, 1)
            dve.wait_ge(pool_consts, 1)

            def list_step(b, j, p):
                o, k = 2 * j + p, TPP * b + 2 * j + p
                order = Order(dve, list_order, passed, k * LIST_LINKS)
                dve.wait_ge(packs_done, 2 * k + 4)
                order.link(nc.vector.scalar_tensor_tensor(key[:, p, :], sums[p], LOWEST,
                                                          column[:, bass.ds(o * STEP_COLS, STEP_COLS)], ALU.is_gt, ALU.mult))
                ins = nc.vector.scalar_tensor_tensor(key[:, p, :], key[:, p, :], float(WORD), sums[p], ALU.mult, ALU.add)
                ins.then_inc(sums_read, 1)
                wait_apart(dve, sums_read, k + 3, passed)
                by_seg = key[:, p, :].rearrange("p (c s) -> p s c", s=SEGS)
                for s in range(SEGS):
                    ins = nc.vector.max(top8[:, p, s, :], by_seg[:, s, :])
                order.link(ins)
                nc.vector.tensor_copy(winners[:, bass.ds(o, 1), :].rearrange("p o c -> p (o c)"),
                                      top8[:, p, :, :].rearrange("p s c -> p (s c)")).then_inc(winners_kept, 1)

            def list_pack(b):
                order = Order(dve, pack_order, passed, b * PACK_LINKS)
                flat_w = winners[:, :, :].rearrange("p o c -> p (o c)")
                dve.wait_ge(winners_kept, TPP * b + TPP)
                order.link(nc.vector.reduce_max(full[:, 0, bass.ds(b, 1)],
                                                flat_w.rearrange("p (n e) -> p n e", e=8)[:, :, 7], AX), apart=True)
                for r in range(SLOTS // 8):
                    order.link(nc.vector.max(slots[:, 8 * r:8 * r + 8], flat_w), apart=True)
                    if r < SLOTS // 8 - 1:
                        order.link(nc.vector.match_replace(flat_w, slots[:, 8 * r:8 * r + 8], flat_w, -1e6), apart=True)
                nc.vector.tensor_copy(full[:, 1, bass.ds(b, 1)], slots[:, SLOTS - 1:SLOTS])
                nc.vector.tensor_scalar(
                    slots_twice[:, :, :], slots[:, :].rearrange("p (o c) -> p o c", o=1).broadcast_to([P, 2, SLOTS]),
                    float(EMPTY), None, ALU.add).then_inc(slots_ready, 1)
                dve.wait_ge(slots_turned, b + 1)
                for g in range(GROUP_COLS):
                    rows = slice(g * SLOTS, (g + 1) * SLOTS)
                    ins = nc.vector.tensor_copy(words[rows, :],
                                                slots_ps[rows, :].rearrange("p (n g) -> p n g", g=GROUP_COLS)[:, :, g])
                    order.link(ins)
                order.link(nc.vector.tensor_scalar(words_less[:, :], words[:, :], -1.0, None, ALU.add))
                nc.vector.tensor_scalar(index[:, :], words_less[:, :], WORD.bit_length() - 1, None,
                                        ALU.logical_shift_right).then_inc(index_ready, 1)
                order.link(nc.vector.tensor_tensor(
                    row_bit[:, :, :], words[:, :].rearrange("p (n o) -> p n o", o=1).broadcast_to([P, SLOTS, BITS]),
                    bit_mask[:, :].rearrange("p (o t) -> p o t", o=1).broadcast_to([P, SLOTS, BITS]), ALU.bitwise_and))

            def make_logits(k, j, p):
                order = Order(dve, attend_order, passed, k * ATTEND_LINKS)
                dve.wait_ge(rows_in[p], 16 * PAIRS * (tile_half(k, j) + 1))
                lg = logits[:, p, :]
                order.link(nc.vector.tensor_tensor(
                    lg.rearrange("p (q t) -> p q t", t=BITS),
                    s1_half[:, bass.ds(k, 1), :].rearrange("p o (q t) -> p (o q) t", t=BITS),
                    gathered[:, p, :, S2:S2 + 1].broadcast_to([P, PAIRS, BITS]), ALU.add))
                order.link(nc.vector.scalar_tensor_tensor(lg, lg, ALPHA, lg, ALU.mult, ALU.max))
                nc.vector.tensor_tensor(lg, lg, m_half[:, bass.ds(k, 1), :].rearrange("p o c -> p (o c)"),
                                        ALU.subtract).then_inc(logits_ready, 1)
                return order

            def make_weights(k, j, p):
                dve.wait_ge(exps_ready, k + 1)
                dve.wait_ge(pv_done, k + 1)
                for g in range(GROUP_COLS):
                    rows = slice(g * SLOTS, (g + 1) * SLOTS)
                    step = P + GROUP_COLS * BITS
                    flat_w = weights[rows, p, :, :].rearrange("p q c -> p (q c)")
                    dst = diagonal(flat_w, g * BITS, step)
                    nc.vector.scalar_tensor_tensor(
                        dst, row_bit[rows, bass.ds((2 * j + p) * PAIRS, PAIRS), :], 0.0,
                        exps[rows, p, :].rearrange("p (q t) -> p q t", t=BITS), ALU.is_gt, ALU.mult)\
                        .then_inc(weights_ready, 1)

            def finish(k, j, p, order):
                dve.wait_ge(pv_done, k + 3)
                nc.vector.tensor_copy(density[:, bass.ds(k, 1)], out_ps[p][:, ONE:ONE + 1])
                nc.vector.reciprocal(recip[:, p:p + 1], out_ps[p][:, ONE:ONE + 1]).then_inc(recip_ready, 1)
                dve.wait_ge(acts_done, k + 3)
                dve.wait_ge(x_again_in[p], 16 * (tile_half(k, j) + 1))
                dve.wait_ge(out_stored[p], 16 * tile_half(k, j) + 16)
                order.link(nc.vector.tensor_scalar(exp_out[:, p, :], exp_out[:, p, :], 1.0, -1.0, ALU.min, ALU.add))
                order.link(nc.vector.tensor_tensor(relu_out[:, p, :], relu_out[:, p, :], x_again[:, p, :], ALU.add))
                nc.vector.tensor_tensor(result[:, p, :], relu_out[:, p, :], exp_out[:, p, :], ALU.add)\
                    .then_inc(result_ready, 1)

            with dve.Fori(0, TPP // 2) as j:
                for p in range(2):
                    list_step(0, j, p)
            list_pack(0)
            with dve.Fori(1, PACKS) as b:
                with dve.Fori(0, TPP // 2) as j:
                    for p in range(2):
                        k = (b - 1) * TPP + 2 * j + p
                        tile_half = lambda k, j, b=b: (b - 1) * (TPP // 2) + j
                        order = make_logits(k, j, p)
                        list_step(b, j, p)
                        make_weights(k, j, p)
                        finish(k, j, p, order)
                list_pack(b)
            with dve.Fori(0, TPP // 2) as j:
                for p in range(2):
                    k = (PACKS - 1) * TPP + 2 * j + p
                    tile_half = lambda k, j: (PACKS - 1) * (TPP // 2) + j
                    order = make_logits(k, j, p)
                    make_weights(k, j, p)
                    finish(k, j, p, order)

            after = Order(dve, setup_order, passed, setup.n)
            after.link(nc.vector.reduce_max(checks[:, 2:3], full[:, :, :].rearrange("p a b -> p (a b)"), AX))
            after.link(nc.vector.tensor_scalar(checks[:, 2:3], checks[:, 2:3], LOWEST, None, ALU.is_gt))
            after.link(nc.vector.tensor_reduce(checks[:, 3:4], density[:, :], AX, ALU.min))
            after.link(nc.vector.tensor_scalar(checks[:, 3:4], checks[:, 3:4], 0.0, None, ALU.is_le))
            after.link(nc.vector.tensor_tensor(checks[:, 4:5], bounds[:, 0:1], bounds[:, 1:2], ALU.add))
            after.link(nc.vector.tensor_scalar(checks[:, 4:5], checks[:, 4:5], SPREAD, None, ALU.is_gt))
            after.link(nc.vector.tensor_tensor(checks[:, 5:6], checks[:, 2:3], checks[:, 3:4], ALU.max))
            nc.vector.tensor_tensor(checks[:, 0:1], checks[:, 5:6], checks[:, 4:5], ALU.max).then_inc(checks_ready, 1)
            dve.wait_ge(flag_ready, 1)
            needed = dve.value_load(flag[0:1, 0:1], min_val=0, max_val=1)
            with dve.If(needed != 0):
                general_vector(dve)
            dve.nop()


PROJ_LINKS = 3
LIST_LINKS = 2
PACK_LINKS = 1 + (SLOTS // 8) + (SLOTS // 8 - 1) + GROUP_COLS + 2
ATTEND_LINKS = 4
GENERAL_LINKS = 11


def diagonal(flat, start, step):
    ap = flat[:, start:start + BITS].rearrange("p (o t) -> p o t", o=1)
    dims = [list(d) for d in ap.ap]
    return bass.AP(tensor=ap.tensor, offset=ap.offset, ap=[dims[0], [step, PAIRS], [1, BITS]])


_INS = ["x", "adj", "L0_gnn_W1", "L0_gnn_b1", "L0_gnn_a1", "L0_gnn_a2", "L0_gnn_b2"]


def kernel(**inputs):
    import concourse.bacc as _bacc
    from concourse.bass_utils import run_bass_kernel_spmd as _run

    nc = _bacc.Bacc("TRN2", target_bir_lowering=False, num_devices=1)
    arrays, args = {}, []
    for name in _INS:
        a = np.ascontiguousarray(inputs[name])
        if a.ndim == 0:
            a = a.reshape(1, 1)
        arrays[name] = a
        args.append(nc.dram_tensor(name, a.shape, mybir.dt.from_np(a.dtype), kind="ExternalInput").ap())
    out = nc.dram_tensor("out", (N, D), F32, kind="ExternalOutput").ap()
    gat_kernel(nc, *args, out)
    return _run(nc, [arrays], core_ids=[0]).results[0]["out"]
```

```python
import numpy as np
import concourse.bass as bass
from concourse import mybir
from contextlib import ExitStack

F32, BF16, I32, I16 = mybir.dt.float32, mybir.dt.bfloat16, mybir.dt.int32, mybir.dt.int16
ALU = mybir.AluOpType
ACT = mybir.ActivationFunctionType
AX = mybir.AxisListType.X
RMAX = bass.bass_isa.ReduceOp.max

P = 128
N, D = 8192, 256
KD = D // P
BITS = 8
PACK_ROWS = P * BITS
PACKS = N // PACK_ROWS
TILES = N // P
TPP = TILES // PACKS
STEP_COLS = N // TPP
SUB = 512
SEGS = 8
SLOTS = P // 2
PAIRS = TPP
GROUP_COLS = 2
WORD = 2 << BITS
EMPTY = (1 << BITS) - 1
LOWEST = 0.5 - EMPTY
S2, ONE = D, D + 1
S1 = D + 1
ROW = D + 1
WIDE = D + 2
ALPHA = 0.2
EPS = 1e-5
MASKED = -1000000000000.0
SPREAD = 60.0
BATCH = 2
BATCHES = TILES // BATCH
BPS = BATCHES // TPP
X_RING = 4
STEPS = TILES
LAG = 9
JB = 8


class Order:

    def __init__(self, eng, sem, passed, start=0):
        self.eng, self.sem, self.passed, self.n = eng, sem, passed, start

    def link(self, instruction, apart=False):
        instruction.then_inc(self.sem, 1)
        self.n = self.n + 1
        if apart:
            wait_apart(self.eng, self.sem, self.n, self.passed)
        else:
            self.eng.wait_ge(self.sem, self.n)


def wait_apart(eng, sem, value, passed):
    eng.wait_ge(sem, value)
    eng.sem_inc(passed, 1)


def gat_kernel(nc, x, adj, W1, b1, a1, a2, b2, out):
    ctx = ExitStack()
    with ctx:
        def sb(name, shape, dt=F32):
            return ctx.enter_context(nc.sbuf_tensor(name, shape, dt))

        def sem(name):
            return ctx.enter_context(nc.semaphore(name))

        table = nc.dram_tensor("table", (N, ROW), F32, kind="Internal").ap()
        s2_dram = nc.dram_tensor("s2_dram", (TILES, P), F32, kind="Internal").ap()

        adj_sb = sb("adj_sb", [P, 4, BITS, SUB], I32)
        signs = sb("signs", [P, 2, BITS, SUB], BF16)
        gathered = sb("gathered", [P, 2, PAIRS, WIDE])
        s1_max = sb("s1_max", [P, 2, TILES, SLOTS])
        column = sb("column", [P, N], I16)
        key = sb("key", [P, 2, STEP_COLS])
        weights = sb("weights", [P, 2, PAIRS, P])
        row_bit = sb("row_bit", [P, 2, PAIRS, BITS], I32)
        bit_mask = sb("bit_mask", [P, BITS], I32)
        top8 = sb("top8", [P, 2, SEGS, 8])
        winners = sb("winners", [P, TPP, SEGS * 8])
        slots = sb("slots", [P, SLOTS])
        slots_twice = sb("slots_twice", [P, 2, SLOTS])
        words = sb("words", [P, PACKS, SLOTS], I32)
        words_less = sb("words_less", [P, SLOTS], I32)
        index = sb("index", [P, PACKS, SLOTS], I32)
        index_now = sb("index_now", [P, 2, PAIRS], I32)
        logits = sb("logits", [P, 2, PAIRS * BITS])
        exps = sb("exps", [P, 2, PAIRS * BITS])
        relu_out = sb("relu_out", [P, 2, D])
        exp_out = sb("exp_out", [P, 2, D])
        x_again = sb("x_again", [P, 2, D])
        result = sb("result", [P, 2, D])
        recip = sb("recip", [P, 2])
        density = sb("density", [P, TILES])
        full = sb("full", [P, 2, PACKS])
        x_in = sb("x_in", [P, X_RING, BATCH, D])
        normed = sb("normed", [P, 2, BATCH, D])
        acts_t = sb("acts_t", [P, 2, KD, BATCH * P])
        stats = sb("stats", [P, 2, BATCH, 6])
        mean_var = sb("mean_var", [P, 2, BATCH, 2])
        std = sb("std", [P, 2, BATCH])
        rstd = sb("rstd", [P, 2, BATCH])
        w_ext = sb("w_ext", [P, KD, WIDE])
        bias_ext = sb("bias_ext", [P, WIDE])
        a_rows = sb("a_rows", [P, 2, D])
        b2_col = sb("b2_col", [P, 1])
        product = sb("product", [P, D])
        u1_rep = sb("u1_rep", [P, KD, P])
        s_cols = sb("s_cols", [P, TILES, 2])
        ident = sb("ident", [P, P])
        ident_bf = sb("ident_bf", [P, P], BF16)
        scaled = sb("scaled", [P, BITS, P], BF16)
        eps_col = sb("eps_col", [P, 1])
        below = sb("below", [P, 1])
        zero_col = sb("zero_col", [P, 1])
        extremes = sb("extremes", [P, 2])
        bounds = sb("bounds", [P, 2])
        checks = sb("checks", [P, 8])
        flag_f = sb("flag_f", [P, 1])
        flag = sb("flag", [P, 1], I32)

        ps = ctx.enter_context(nc.psum_tensor("ps", [P, 8, SUB], F32))
        sums = [ps[:, 2 * q:2 * q + 2, :].rearrange("p k c -> p (k c)") for q in range(2)]
        slots_ps = ps[:, 6, 0:P]
        out_ps = [ps[:, 4 + q, 0:WIDE] for q in range(2)]
        h_ps = ps[:, 4:4 + BATCH, 0:WIDE]
        s1_ps = ps[:, 6, 0:BATCH * P]
        turned = ps[:, 7, :]

        adj_in = [sem(f"adj_in{i}") for i in range(4)]
        signs_done = sem("signs_done")
        packs_done = sem("packs_done")
        sums_read = sem("sums_read")
        winners_kept = sem("winners_kept")
        slots_ready = sem("slots_ready")
        slots_turned = sem("slots_turned")
        index_ready = sem("index_ready")
        index_copied = sem("index_copied")
        rows_in = [sem(f"rows_in{i}") for i in range(2)]
        logits_ready = sem("logits_ready")
        exps_ready = sem("exps_ready")
        weights_ready = sem("weights_ready")
        pv_done = sem("pv_done")
        recip_ready = sem("recip_ready")
        acts_done = sem("acts_done")
        x_again_in = [sem(f"x_again_in{i}") for i in range(2)]
        result_ready = sem("result_ready")
        out_stored = [sem(f"out_stored{i}") for i in range(2)]
        key_order = sem("key_order")
        top8_order = sem("top8_order")
        pack_order = sem("pack_order")
        logits_order = sem("logits_order")
        bits_order = sem("bits_order")
        finish_order = sem("finish_order")
        x_in_sem = [sem(f"x_in{i}") for i in range(X_RING)]
        params_in = sem("params_in")
        ident_ready = sem("ident_ready")
        pool_consts = sem("pool_consts")
        scaled_ready = sem("scaled_ready")
        setup_order = sem("setup_order")
        stats_order = sem("stats_order")
        rstd_order = sem("rstd_order")
        rows_order = sem("rows_order")
        var_ready = sem("var_ready")
        std_ready = sem("std_ready")
        normed_ready = sem("normed_ready")
        turned_ready = sem("turned_ready")
        acts_t_ready = sem("acts_t_ready")
        h_ready = sem("h_ready")
        h_read = sem("h_read")
        table_stored = [sem(f"table_stored{i}") for i in range(2)]
        extremes_ready = sem("extremes_ready")
        bounds_ready = sem("bounds_ready")
        attend_ready = sem("attend_ready")
        checks_ready = sem("checks_ready")
        checks_done = sem("checks_done")
        flag_ready = sem("flag_ready")
        passed = sem("passed")
        g_turn = sem("g_turn")
        g_s2 = sem("g_s2")
        g_s2_stored = sem("g_s2_stored")
        g_s2_in = sem("g_s2_in")
        g_order = sem("g_order")
        g_row_in = sem("g_row_in")
        g_scores = sem("g_scores")
        g_exps = sem("g_exps")
        g_h_in = sem("g_h_in")
        g_block = sem("g_block")
        g_block_ps = sem("g_block_ps")
        g_block_t = sem("g_block_t")
        g_part = sem("g_part")
        g_added = sem("g_added")
        g_low = sem("g_low")
        g_exp_out = sem("g_exp_out")
        g_result = sem("g_result")
        g_stored = sem("g_stored")

        adj_v = adj.rearrange("(b g t) (o s c) -> b o s g t c", g=P, t=BITS, s=2, c=SUB)
        x_batch = x.rearrange("(m i p) f -> m p i f", i=BATCH, p=P)
        table_batch = table.rearrange("(m i p) f -> m p i f", i=BATCH, p=P)
        x_tile = x.rearrange("(k p) f -> k p f", p=P)
        out_tile = out.rearrange("(k p) f -> k p f", p=P)

        h_sb = [gathered[:, q, 0:BATCH, :] for q in range(2)]
        s1_half = s1_max[:, 0, :, :]
        m_half = s1_max[:, 1, :, :]

        flat = adj_sb[:, :, :, :].rearrange("p a t c -> p (a t c)")
        g_row, g_rowf = flat[:, 0:N], flat[:, 0:N].bitcast(F32)
        g_e = flat[:, N:2 * N].bitcast(F32)
        g_s2b = s1_max[:, :, :, :].rearrange("p a t c -> p (a t c)")
        g_h = gathered[:, :, :, :].rearrange("p a t c -> p (a t c)")[:, 0:JB * D].rearrange("p (j f) -> p j f", j=JB)
        g_blk, g_blk_t = weights[:, 0, 0, :], weights[:, 0, 1, :]
        g_acc = weights[:, 1, 0:2, :].rearrange("p a c -> p (a c)")
        table_jb = table.rearrange("(b j p) f -> b p j f", j=JB, p=P)

        block = ctx.enter_context(nc.Block())

        def general_loads(sp):
            sp.wait_ge(g_s2, 1)
            sp.dma_start(s2_dram, product[0:TILES, 0:P]).then_inc(g_s2_stored, 16)
            sp.wait_ge(g_s2_stored, 16)
            sp.dma_start(g_s2b, s2_dram.rearrange("(o i) p -> o (i p)", o=1).broadcast_to([P, N])).then_inc(g_s2_in, 16)
            with sp.Fori(0, TILES) as i:
                wait_apart(sp, g_scores, i + 1, passed)
                wait_apart(sp, g_stored, 16 * i + 16, passed)
                sp.dma_start(g_row, adj.rearrange("(i p) n -> i p n", p=P)[i]).then_inc(g_row_in, 16)
                sp.dma_start(x_again[:, 0, :], x_tile[i]).then_inc(g_row_in, 16)
                with sp.Fori(0, TILES // JB) as jb:
                    wait_apart(sp, g_part, i * TILES + jb * JB + 1, passed)
                    sp.dma_start(g_h, table_jb[jb][:, :, 0:D]).then_inc(g_h_in, 16)
                wait_apart(sp, g_result, i + 1, passed)
                sp.dma_start(out_tile[i], result[:, 0, :]).then_inc(g_stored, 16)
            wait_apart(sp, g_stored, 16 * TILES + 16, passed)

        def general_scalar(act):
            with act.Fori(0, TILES) as i:
                act.wait_ge(g_scores, i + 2)
                nc.scalar.activation(g_e, g_e, ACT.Exp, bias=checks[:, 1:2], accum_out=checks[:, 2:3]).then_inc(g_exps, 1)
                act.wait_ge(g_low, i + 1)
                nc.scalar.activation(exp_out[:, 0, :], exp_out[:, 0, :], ACT.Exp, bias=zero_col[:, :]).then_inc(g_exp_out, 1)

        def general_tensor(pe):
            nc.tensor.transpose(ps[0:TILES, 0, 0:P], s_cols[:, :, 0], ident[:, :]).then_inc(g_turn, 1)
            with pe.Fori(0, TILES) as i:
                with pe.Fori(0, TILES // JB) as jb:
                    for jj in range(JB):
                        u = i * TILES + jb * JB + jj
                        pe.wait_ge(g_block, u + 1)
                        nc.tensor.transpose(ps[:, 1, 0:P], g_blk, ident[:, :]).then_inc(g_block_ps, 1)
                        pe.wait_ge(g_block_t, u + 1)
                        pe.wait_ge(g_h_in, 16 * (i * (TILES // JB) + jb + 1))
                        nc.tensor.matmul(ps[:, 2, 0:D], g_blk_t, g_h[:, jj, :], start=True, stop=True).then_inc(g_part, 1)

        def general_vector(dve):
            dve.sem_inc(g_scores, 1)
            dve.sem_inc(g_stored, 16)
            dve.sem_inc(g_part, 1)
            dve.wait_ge(g_turn, 1)
            nc.vector.tensor_copy(product[0:TILES, 0:P], ps[0:TILES, 0, 0:P]).then_inc(g_s2, 1)
            dve.wait_ge(g_s2_in, 16)
            with dve.Fori(0, TILES) as i:
                order = Order(dve, g_order, passed, i * GENERAL_LINKS)
                dve.wait_ge(g_row_in, 32 * i + 32)
                dve.wait_ge(g_part, i * TILES + 1)
                order.link(nc.vector.tensor_copy(checks[:, 0:1], s_cols[:, bass.ds(i, 1), 1]))
                order.link(nc.vector.tensor_scalar(g_e, g_s2b, checks[:, 0:1], None, ALU.add))
                order.link(nc.vector.scalar_tensor_tensor(g_e, g_e, ALPHA, g_e, ALU.mult, ALU.max))
                order.link(nc.vector.scalar_tensor_tensor(g_e, g_row, 0.0, g_e, ALU.is_gt, ALU.mult))
                order.link(nc.vector.tensor_scalar(g_rowf, g_row, 0.0, MASKED, ALU.is_le, ALU.mult))
                order.link(nc.vector.tensor_tensor(g_e, g_e, g_rowf, ALU.add))
                order.link(nc.vector.reduce_max(checks[:, 3:4], g_e, AX))
                order.link(nc.vector.memset(g_acc, 0.0))
                nc.vector.tensor_scalar(checks[:, 1:2], checks[:, 3:4], -1.0, None, ALU.mult).then_inc(g_scores, 1)
                wait_apart(dve, g_exps, i + 1, passed)
                order.link(nc.vector.reciprocal(checks[:, 4:5], checks[:, 2:3]), apart=True)
                with dve.Fori(0, TILES // JB) as jb:
                    for jj in range(JB):
                        u = i * TILES + jb * JB + jj
                        nc.vector.tensor_copy(g_blk, g_e[:, bass.ds((jb * JB + jj) * P, P)]).then_inc(g_block, 1)
                        dve.wait_ge(g_block_ps, u + 1)
                        nc.vector.tensor_copy(g_blk_t, ps[:, 1, 0:P]).then_inc(g_block_t, 1)
                        dve.wait_ge(g_part, u + 2)
                        nc.vector.tensor_tensor(g_acc, g_acc, ps[:, 2, 0:D], ALU.add).then_inc(g_added, 1)
                        dve.wait_ge(g_added, u + 1)
                dve.wait_ge(g_stored, 16 * i + 16)
                order.link(nc.vector.tensor_scalar(relu_out[:, 0, :], g_acc, checks[:, 4:5], 0.0, ALU.mult, ALU.max))
                nc.vector.tensor_scalar(exp_out[:, 0, :], g_acc, checks[:, 4:5], 0.0, ALU.mult, ALU.min).then_inc(g_low, 1)
                dve.wait_ge(g_exp_out, i + 1)
                order.link(nc.vector.scalar_tensor_tensor(exp_out[:, 0, :], exp_out[:, 0, :], -1.0, relu_out[:, 0, :],
                                                          ALU.add, ALU.add))
                nc.vector.tensor_tensor(result[:, 0, :], exp_out[:, 0, :], x_again[:, 0, :], ALU.add).then_inc(g_result, 1)

        def is_first_pack(b):
            return isinstance(b, int) and b == 0

        def real(tile, b):
            return not is_first_pack(b) and (not isinstance(tile, int) or 0 <= tile < TILES)

        def all_steps(eng, step, pack_end):
            step(0, 0, 0, 0)
            with eng.Fori(0, TPP // 2 - 1) as j:
                step(2 * j + 1, 0, 2 * j + 1, 1)
                step(2 * j + 2, 0, 2 * j + 2, 0)
            step(TPP - 1, 0, TPP - 1, 1)
            pack_end(0)
            for o in range(4):
                step(TPP + o, 1, o, o % 2)
            with eng.Fori(2, TPP // 2) as j:
                for p in range(2):
                    step(2 * j + p + TPP, 1, 2 * j + p, p)
            pack_end(1)
            with eng.Fori(2, PACKS) as b:
                for p in range(2):
                    step(b * TPP + p, b, p, p)
                with eng.Fori(1, TPP // 2) as j:
                    for p in range(2):
                        step(b * TPP + 2 * j + p, b, 2 * j + p, p)
                pack_end(b)
            for p in range(2):
                step(STEPS + p, None, p, p)
            with eng.Fori(1, TPP // 2) as j:
                for p in range(2):
                    step(2 * j + p + STEPS, None, 2 * j + p, p)
            for o in range(4):
                step(STEPS + TPP + o, None, TPP + o, o % 2)

        def pair_value(t, q, per_use, uses=1):
            return (t - q) * (per_use // 2) + uses * per_use

        @block.sync
        def _(sp):
            sp.dma_start(w_ext[:, :, 0:D], W1.rearrange("(k p) f -> p k f", p=P)).then_inc(params_in, 16)
            sp.dma_start(a_rows[:, 0, :], a1.rearrange("(o f) -> o f", o=1).broadcast_to([P, D])).then_inc(params_in, 16)
            sp.dma_start(a_rows[:, 1, :], a2.rearrange("(o f) -> o f", o=1).broadcast_to([P, D])).then_inc(params_in, 16)
            sp.dma_start(bias_ext[:, 0:D], b1.rearrange("(o f) -> o f", o=1).broadcast_to([P, D])).then_inc(params_in, 16)
            sp.dma_start(b2_col[:, :], b2.broadcast_to([P, 1])).then_inc(params_in, 16)

            def step(k, b, o, p):
                if b is None:
                    return
                for s in range(2):
                    i = 2 * p + s
                    wait_apart(sp, signs_done, 2 * k + s + 1, passed)
                    sp.dma_start(adj_sb[:, i, :, :], adj_v[b, o, s]).then_inc(adj_in[i], 16)

            def step_loops():
                with sp.Fori(0, PACKS) as b:
                    with sp.Fori(0, TPP // 2) as j:
                        for p in range(2):
                            step(b * TPP + 2 * j + p, b, 2 * j + p, p)

            step_loops()
            sp.wait_ge(flag_ready, 1)
            needed = sp.value_load(flag[0:1, 0:1], min_val=0, max_val=1)
            with sp.If(needed != 0):
                general_loads(sp)
            sp.nop()

        @block.gpsimd
        def _(pool):
            pool.memset(ident[:, :], 0.0).then_inc(ident_ready, 1)
            pool.iota(column[:, :], pattern=[[1, N]], base=0, channel_multiplier=0).then_inc(pool_consts, 1)
            pool.wait_ge(ident_ready, 1)
            pool.affine_select(out=ident[:, :], in_=ident[:, :], compare_op=ALU.not_equal, fill=1.0, base=0,
                               pattern=[[-1, P]], channel_multiplier=1).then_inc(ident_ready, 1)
            with pool.Fori(0, BATCHES // 2) as m:
                for q in range(2):
                    wait_apart(pool, h_read, 2 * m + q + 2, passed)
                    pool.dma_start(table_batch[2 * m + q], h_sb[q][:, :, 0:ROW]).then_inc(table_stored[q], 16)
            pool.wait_ge(extremes_ready, 1)
            pool.partition_all_reduce(bounds[:, :], extremes[:, :], P, RMAX).then_inc(bounds_ready, 1)
            for q in range(2):
                pool.wait_ge(table_stored[q], 16 * (BATCHES // 2))
            pool.wait_ge(attend_ready, 1)

            with pool.Fori(0, PACKS) as b:
                wait_apart(pool, index_ready, b + 1, passed)
                with pool.Fori(0, TPP // 2) as j:
                    for p in range(2):
                        k = b * TPP + 2 * j + p
                        pool.wait_ge(pv_done, k + 1)
                        pool.tensor_copy(index_now[:, p, :], index[:, b, bass.ds((2 * j + p) * PAIRS, PAIRS)])\
                            .then_inc(index_copied, 1)
                        wait_apart(pool, index_copied, k + 1, passed)
                        for q in range(PAIRS):
                            pool.indirect_dma_start(
                                out=gathered[:, p, q, 0:ROW], out_offset=None, in_=table,
                                in_offset=bass.IndirectOffsetOnAxis(ap=index_now[:, p, q:q + 1], axis=0),
                                bounds_check=N - 1, oob_is_err=False).then_inc(rows_in[p], 16)
            pool.wait_ge(checks_ready, 1)
            pool.partition_all_reduce(flag_f[:, :], checks[:, 0:1], P, RMAX).then_inc(checks_done, 1)
            pool.wait_ge(checks_done, 1)
            pool.tensor_copy(flag[:, :], flag_f[:, :]).then_inc(flag_ready, 1)

        @block.scalar
        def _(act):
            act.sem_inc(acts_done, 2)
            act.sem_inc(signs_done, 4)

            def load_x(u, ring):
                act.dma_start(x_in[:, ring, :, :], x_batch[u]).then_inc(x_in_sem[ring], 16)

            def take_signs(k, p, s):
                i = 2 * p + s
                act.wait_ge(adj_in[i], pair_value(k, p, 16))
                act.wait_ge(packs_done, 2 * k + s + 1)
                nc.scalar.activation(signs[:, s, :, :], adj_sb[:, i, :, :], ACT.Sign,
                                     bias=below[:, :]).then_inc(signs_done, 1)

            def slot(u, q, ring, last):
                if not last:
                    deviation(u + 1, 1 - q)
                act.wait_ge(turned_ready, u + 3)
                act.wait_ge(h_ready, u + 1)
                nc.scalar.activation(acts_t[:, q, :, :].rearrange("p k c -> p (k c)"), turned, ACT.Relu)\
                    .then_inc(acts_t_ready, 1)

            def deviation(u, q):
                act.wait_ge(var_ready, u + 1)
                nc.scalar.activation(std[:, q, :], mean_var[:, q, :, 1], ACT.Sqrt, bias=eps_col[:, :])\
                    .then_inc(std_ready, 1)

            def step(k, b, o, p):
                t = k - (LAG + 1)
                if real(t, b):
                    act_exps = (t, (p + LAG + 1) % 2)
                if b is not None:
                    take_signs(k, p, 0)
                if real(t, b):
                    exponents(*act_exps)
                if b is not None:
                    take_signs(k, p, 1)
                if is_first_pack(b):
                    for i in range(BPS):
                        last = isinstance(k, int) and BPS * k + i == BATCHES - 1
                        slot(k * BPS + i, i % 2, i, last)
                        if not (isinstance(k, int) and BPS * k + i + X_RING >= BATCHES):
                            load_x(k * BPS + i + X_RING, i)
                t, q = k - (LAG + 2), (p + LAG + 2) % 2
                if real(t, b):
                    fetch_x(t, q)
                    normalise(t, q)
                t, q = k - (LAG + 3), (p + LAG + 3) % 2
                if real(t, b):
                    store(t, q)

            def fetch_x(t, q):
                act.wait_ge(result_ready, t + 1)
                act.dma_start(x_again[:, q, :], x_tile[t]).then_inc(x_again_in[q], 16)

            def exponents(t, q):
                act.wait_ge(logits_ready, t + 1)
                nc.scalar.activation(exps[:, q, :], logits[:, q, :], ACT.Exp, bias=zero_col[:, :]).then_inc(exps_ready, 1)

            def normalise(t, q):
                act.wait_ge(recip_ready, t + 1)
                nc.scalar.activation(relu_out[:, q, :], out_ps[q][:, 0:D], ACT.Relu, scale=recip[:, q:q + 1])
                nc.scalar.activation(exp_out[:, q, :], out_ps[q][:, 0:D], ACT.Exp, bias=zero_col[:, :],
                                     scale=recip[:, q:q + 1]).then_inc(acts_done, 1)

            def store(t, q):
                act.wait_ge(result_ready, t + 3)
                act.dma_start(out_tile[t], result[:, q, :]).then_inc(out_stored[q], 16)

            for u in range(X_RING):
                load_x(u, u)
            deviation(0, 0)
            all_steps(act, step, lambda b: None)
            for p in range(2):
                act.wait_ge(out_stored[p], 16 * (TILES // 2) + 16)
            act.wait_ge(flag_ready, 1)
            needed = act.value_load(flag[0:1, 0:1], min_val=0, max_val=1)
            with act.If(needed != 0):
                general_scalar(act)
            act.nop()

        @block.tensor
        def _(pe):
            pe.sem_inc(turned_ready, 2)
            pe.sem_inc(h_ready, 2)
            pe.sem_inc(packs_done, 2)
            pe.sem_inc(pv_done, 2)
            pe.wait_ge(ident_ready, 2)
            pe.wait_ge(scaled_ready, BITS)

            def turn(u, q):
                pe.wait_ge(normed_ready, u + 1)
                pe.wait_ge(acts_t_ready, u + 1)
                for k in range(KD):
                    for i in range(BATCH):
                        last = nc.tensor.transpose(turned[:, (k * BATCH + i) * P:(k * BATCH + i + 1) * P],
                                                   normed[:, q, i, k * P:(k + 1) * P], ident[:, :])
                last.then_inc(turned_ready, 1)

            def project(u, q):
                pe.wait_ge(acts_t_ready, u + 2)
                pe.wait_ge(h_read, u + 1)
                for k in range(KD):
                    nc.tensor.matmul(s1_ps, u1_rep[:, k, :], acts_t[:, q, k, :], start=(k == 0), stop=(k == KD - 1))
                for i in range(BATCH):
                    for k in range(KD):
                        last = nc.tensor.matmul(h_ps[:, i, :], acts_t[:, q, k, i * P:(i + 1) * P], w_ext[:, k, :],
                                                start=(k == 0), stop=(k == KD - 1))
                last.then_inc(h_ready, 1)

            def add_signs(k, p):
                pe.wait_ge(sums_read, k + 1)
                for s in range(2):
                    pe.wait_ge(signs_done, 2 * k + s + 5)
                    for t in range(BITS):
                        last = nc.tensor.matmul(sums[p][:, s * SUB:(s + 1) * SUB], scaled[:, t, :], signs[:, s, t, :],
                                                start=(t == 0), stop=(t == BITS - 1))
                    last.then_inc(packs_done, 1)

            def turn_slots(b):
                pe.wait_ge(slots_ready, b + 1)
                nc.tensor.transpose(slots_ps, slots_twice[:, :, :].rearrange("p a c -> p (a c)"), ident[:, :])\
                    .then_inc(slots_turned, 1)

            def weigh(t, q):
                pe.wait_ge(weights_ready, 2 * t + 2)
                pe.wait_ge(acts_done, t + 1)
                for i in range(PAIRS):
                    last = nc.tensor.matmul(out_ps[q], weights[:, q, i, :], gathered[:, q, i, :],
                                            start=(i == 0), stop=(i == PAIRS - 1))
                last.then_inc(pv_done, 1)

            def step(k, b, o, p):
                if b is not None:
                    add_signs(k, p)
                if isinstance(o, int) and o == 0 and not is_first_pack(b):
                    turn_slots(PACKS - 1 if b is None else b - 1)
                if is_first_pack(b):
                    for i in range(BPS):
                        u = k * BPS + i
                        turn(u, i % 2)
                        if not (isinstance(u, int) and u == 0):
                            project(u - 1, 1 - i % 2)
                t, q = k - (LAG + 1), (p + LAG + 1) % 2
                if real(t, b):
                    weigh(t, q)

            def pack_end(b):
                if is_first_pack(b):
                    project(BATCHES - 1, (BATCHES - 1) % 2)
                    pe.wait_ge(h_read, BATCHES + 1)

            all_steps(pe, step, pack_end)
            pe.wait_ge(flag_ready, 1)
            needed = pe.value_load(flag[0:1, 0:1], min_val=0, max_val=1)
            with pe.If(needed != 0):
                general_tensor(pe)
            pe.nop()

        @block.vector
        def _(dve):
            dve.sem_inc(h_read, 1)
            for q in range(2):
                dve.sem_inc(out_stored[q], 16)
            dve.sem_inc(sums_read, 2)
            dve.sem_inc(result_ready, 2)
            dve.sem_inc(acts_t_ready, 1)
            nc.vector.memset(eps_col[:, :], EPS)
            nc.vector.memset(below[:, :], -0.5)
            nc.vector.memset(zero_col[:, :], 0.0)
            nc.vector.memset(weights[:, :, :, :], 0.0)
            for t in range(BITS):
                nc.vector.memset(bit_mask[:, t:t + 1], 2 << t)
            dve.wait_ge(ident_ready, 2)
            for t in range(BITS):
                nc.vector.tensor_scalar(scaled[:, t, :], ident[:, :], float(1 << t), None, ALU.mult)\
                    .then_inc(scaled_ready, 1)
            dve.wait_ge(params_in, 80)
            setup = Order(dve, setup_order, passed)
            for c, a in ((S2, 1), (S1, 0)):
                for k in range(KD):
                    setup.link(nc.vector.tensor_tensor(product[:, :], w_ext[:, k, 0:D], a_rows[:, a, :], ALU.mult))
                    setup.link(nc.vector.reduce_sum(w_ext[:, k, c:c + 1], product[:, :], AX))
                setup.link(nc.vector.tensor_tensor(product[:, :], bias_ext[:, 0:D], a_rows[:, a, :], ALU.mult))
                setup.link(nc.vector.reduce_sum(bias_ext[:, c:c + 1], product[:, :], AX))
            setup.link(nc.vector.tensor_tensor(bias_ext[:, S1:S1 + 1], bias_ext[:, S1:S1 + 1], b2_col[:, :], ALU.add))
            for k in range(KD):
                setup.link(nc.vector.tensor_copy(u1_rep[:, k, :], w_ext[:, k, S1:S1 + 1].broadcast_to([P, P])))

            def take_stats(u, q, ring):
                dve.wait_ge(x_in_sem[ring], ring_value(u, ring))
                for i in range(BATCH):
                    last = nc.vector.bn_stats(stats[:, q, i, :], x_in[:, ring, i, :])
                last.then_inc(stats_order, 1)
                wait_apart(dve, stats_order, u + 1, passed)
                for i in range(BATCH):
                    last = nc.vector.bn_aggr(mean_var[:, q, i, :], stats[:, q, i, :])
                last.then_inc(var_ready, 1)

            def ring_value(u, ring):
                return (u - ring) * (16 // X_RING) + 16

            def norm(u, q, ring):
                dve.wait_ge(std_ready, u + 1)
                nc.vector.reciprocal(rstd[:, q, :], std[:, q, :]).then_inc(rstd_order, 1)
                dve.wait_ge(rstd_order, u + 1)
                dve.wait_ge(turned_ready, u + 1)
                for i in range(BATCH):
                    last = nc.vector.tensor_scalar(normed[:, q, i, :], x_in[:, ring, i, :], mean_var[:, q, i, 0:1],
                                                   rstd[:, q, i:i + 1], ALU.subtract, ALU.mult)
                last.then_inc(normed_ready, 1)

            def take_rows(u, q):
                dve.wait_ge(h_ready, u + 3)
                if not (isinstance(u, int) and u < 2):
                    dve.wait_ge(table_stored[q], pair_value(u, q, 16, uses=0))
                nc.vector.tensor_tensor(
                    h_sb[q], h_ps, bias_ext[:, :].rearrange("p (o f) -> p o f", o=1).broadcast_to([P, BATCH, WIDE]),
                    ALU.add).then_inc(rows_order, 1)
                for g in range(GROUP_COLS):
                    rows = slice(g * SLOTS, (g + 1) * SLOTS)
                    nc.vector.tensor_scalar(
                        s1_half[rows, bass.ds(u * BATCH, BATCH), :].rearrange("p i (q t) -> p (i q) t", t=BITS),
                        s1_ps[rows, :].rearrange("p (n g t) -> p n g t", g=GROUP_COLS, t=BITS)[:, :, g, :],
                        bias_ext[rows, S1:S1 + 1], None, ALU.add)
                dve.wait_ge(rows_order, u + 1)
                nc.vector.tensor_copy(s_cols[:, bass.ds(u * BATCH, BATCH), :], h_sb[q][:, :, S2:S2 + 2]).then_inc(h_read, 1)

            def end_projection():
                take_rows(BATCHES - 2, 0)
                take_rows(BATCHES - 1, 1)
                dve.wait_ge(h_read, BATCHES + 1)
                setup.link(nc.vector.reduce_max(extremes[:, 0:1], s_cols[:, :, 0], AX))
                setup.link(nc.vector.tensor_reduce(checks[:, 1:2], s_cols[:, :, 0], AX, ALU.min))
                nc.vector.tensor_scalar(extremes[:, 1:2], checks[:, 1:2], -1.0, None, ALU.mult).then_inc(extremes_ready, 1)
                dve.wait_ge(bounds_ready, 1)
                flat_s1 = s1_half.rearrange("p i c -> p (i c)")
                flat_m = m_half.rearrange("p i c -> p (i c)")
                setup.link(nc.vector.tensor_scalar(flat_m, flat_s1, bounds[:, 0:1], None, ALU.add))
                setup.link(nc.vector.scalar_tensor_tensor(flat_m, flat_m, ALPHA, flat_m, ALU.mult, ALU.max))
                for q in range(2):
                    dve.wait_ge(table_stored[q], 16 * (BATCHES // 2))
                setup.link(nc.vector.memset(gathered[:, :, :, 0:D], 0.0))
                setup.link(nc.vector.memset(gathered[:, :, :, S2:S2 + 1], -1e30))
                nc.vector.memset(gathered[:, :, :, ONE:ONE + 1], 1.0).then_inc(attend_ready, 1)

            def list_step(k, o, p):
                dve.wait_ge(packs_done, 2 * k + 4)
                nc.vector.scalar_tensor_tensor(key[:, p, :], sums[p], LOWEST, column[:, bass.ds(o * STEP_COLS, STEP_COLS)],
                                               ALU.is_gt, ALU.mult).then_inc(key_order, 1)
                dve.wait_ge(key_order, k + 1)
                nc.vector.scalar_tensor_tensor(key[:, p, :], key[:, p, :], float(WORD), sums[p], ALU.mult, ALU.add)\
                    .then_inc(sums_read, 1)
                wait_apart(dve, sums_read, k + 3, passed)
                by_seg = key[:, p, :].rearrange("p (c s) -> p s c", s=SEGS)
                for s in range(SEGS):
                    last = nc.vector.max(top8[:, p, s, :], by_seg[:, s, :])
                last.then_inc(top8_order, 1)

            def keep_winners(k, o, p):
                dve.wait_ge(top8_order, k + 1)
                nc.vector.tensor_copy(winners[:, bass.ds(o, 1), :].rearrange("p o c -> p (o c)"),
                                      top8[:, p, :, :].rearrange("p s c -> p (s c)")).then_inc(winners_kept, 1)

            def list_pack(b):
                order = Order(dve, pack_order, passed, b * PACK_LINKS)
                flat_w = winners[:, :, :].rearrange("p o c -> p (o c)")
                dve.wait_ge(winners_kept, TPP * b + TPP)
                order.link(nc.vector.reduce_max(full[:, 0, bass.ds(b, 1)],
                                                flat_w.rearrange("p (n e) -> p n e", e=8)[:, :, 7], AX), apart=True)
                for r in range(SLOTS // 8):
                    order.link(nc.vector.max(slots[:, 8 * r:8 * r + 8], flat_w), apart=True)
                    if r < SLOTS // 8 - 1:
                        order.link(nc.vector.match_replace(flat_w, slots[:, 8 * r:8 * r + 8], flat_w, -1e6), apart=True)
                nc.vector.tensor_copy(full[:, 1, bass.ds(b, 1)], slots[:, SLOTS - 1:SLOTS])
                nc.vector.tensor_scalar(
                    slots_twice[:, :, :], slots[:, :].rearrange("p (o c) -> p o c", o=1).broadcast_to([P, 2, SLOTS]),
                    float(EMPTY), None, ALU.add).then_inc(slots_ready, 1)
                dve.wait_ge(slots_turned, b + 1)
                for g in range(GROUP_COLS):
                    rows = slice(g * SLOTS, (g + 1) * SLOTS)
                    order.link(nc.vector.tensor_copy(words[rows, b, :],
                                                     slots_ps[rows, :].rearrange("p (n g) -> p n g", g=GROUP_COLS)[:, :, g]))
                order.link(nc.vector.tensor_scalar(words_less[:, :], words[:, b, :], -1.0, None, ALU.add))
                nc.vector.tensor_scalar(index[:, b, :], words_less[:, :], WORD.bit_length() - 1, None,
                                        ALU.logical_shift_right).then_inc(index_ready, 1)

            words_by_tile = words[:, :, :].rearrange("p b (i q) -> p (b i) q", q=PAIRS)

            def make_logits(t, q):
                order = Order(dve, logits_order, passed, t * LOGITS_LINKS)
                dve.wait_ge(rows_in[q], pair_value(t, q, 16 * PAIRS))
                lg = logits[:, q, :]
                order.link(nc.vector.tensor_tensor(
                    lg.rearrange("p (i t) -> p i t", t=BITS),
                    s1_half[:, bass.ds(t, 1), :].rearrange("p o (i t) -> p (o i) t", t=BITS),
                    gathered[:, q, :, S2:S2 + 1].broadcast_to([P, PAIRS, BITS]), ALU.add))
                order.link(nc.vector.scalar_tensor_tensor(lg, lg, ALPHA, lg, ALU.mult, ALU.max))
                nc.vector.tensor_tensor(lg, lg, m_half[:, bass.ds(t, 1), :].rearrange("p o c -> p (o c)"),
                                        ALU.subtract).then_inc(logits_ready, 1)
                nc.vector.tensor_tensor(
                    row_bit[:, q, :, :],
                    words_by_tile[:, bass.ds(t, 1), :].rearrange("p o i -> p (o i)").rearrange("p (i o) -> p i o", o=1)
                    .broadcast_to([P, PAIRS, BITS]),
                    bit_mask[:, :].rearrange("p (o t) -> p o t", o=1).broadcast_to([P, PAIRS, BITS]),
                    ALU.bitwise_and).then_inc(bits_order, 1)

            def make_weights(t, q):
                dve.wait_ge(exps_ready, t + 1)
                dve.wait_ge(bits_order, t + 1)
                dve.wait_ge(pv_done, t + 1)
                for g in range(GROUP_COLS):
                    rows = slice(g * SLOTS, (g + 1) * SLOTS)
                    nc.vector.scalar_tensor_tensor(
                        diagonal(weights[rows, q, :, :].rearrange("p i c -> p (i c)"), g * BITS, P + GROUP_COLS * BITS),
                        row_bit[rows, q, :, :], 0.0,
                        exps[rows, q, :].rearrange("p (i t) -> p i t", t=BITS), ALU.is_gt, ALU.mult)\
                        .then_inc(weights_ready, 1)

            def invert(t, q):
                dve.wait_ge(pv_done, t + 3)
                nc.vector.tensor_copy(density[:, bass.ds(t, 1)], out_ps[q][:, ONE:ONE + 1])
                nc.vector.reciprocal(recip[:, q:q + 1], out_ps[q][:, ONE:ONE + 1]).then_inc(recip_ready, 1)

            def finish(t, q):
                order = Order(dve, finish_order, passed, t * FINISH_LINKS)
                dve.wait_ge(acts_done, t + 3)
                dve.wait_ge(x_again_in[q], pair_value(t, q, 16))
                dve.wait_ge(out_stored[q], pair_value(t, q, 16))
                nc.vector.tensor_scalar(exp_out[:, q, :], exp_out[:, q, :], 1.0, -1.0, ALU.min, ALU.add)
                order.link(nc.vector.tensor_tensor(relu_out[:, q, :], relu_out[:, q, :], x_again[:, q, :], ALU.add))
                nc.vector.tensor_tensor(result[:, q, :], relu_out[:, q, :], exp_out[:, q, :], ALU.add)\
                    .then_inc(result_ready, 1)

            def step(k, b, o, p):
                t, q = k - LAG, (p + LAG) % 2
                if real(t, b):
                    make_logits(t, q)
                if is_first_pack(b):
                    for i in range(BPS):
                        u = k * BPS + i
                        if not (isinstance(u, int) and u == BATCHES - 1):
                            take_stats(u + 1, 1 - i % 2, (i + 1) % X_RING)
                        norm(u, i % 2, i)
                        if not (isinstance(u, int) and u < 2):
                            take_rows(u - 2, i % 2)
                        if i == 1:
                            list_step(k, o, p)
                    keep_winners(k, o, p)
                elif b is not None:
                    list_step(k, o, p)
                if real(t - 1, b):
                    invert(t - 1, 1 - q)
                if real(t, b):
                    make_weights(t, q)
                if real(t - 2, b):
                    finish(t - 2, q)
                if b is not None and not is_first_pack(b):
                    keep_winners(k, o, p)

            def pack_end(b):
                if is_first_pack(b):
                    end_projection()
                list_pack(b)

            take_stats(0, 0, 0)
            dve.wait_ge(pool_consts, 1)
            all_steps(dve, step, pack_end)

            after = Order(dve, setup_order, passed, setup.n)
            after.link(nc.vector.reduce_max(checks[:, 2:3], full[:, :, :].rearrange("p a b -> p (a b)"), AX))
            after.link(nc.vector.tensor_scalar(checks[:, 2:3], checks[:, 2:3], LOWEST, None, ALU.is_gt))
            after.link(nc.vector.tensor_reduce(checks[:, 3:4], density[:, :], AX, ALU.min))
            after.link(nc.vector.tensor_scalar(checks[:, 3:4], checks[:, 3:4], 0.0, None, ALU.is_le))
            after.link(nc.vector.tensor_tensor(checks[:, 4:5], bounds[:, 0:1], bounds[:, 1:2], ALU.add))
            after.link(nc.vector.tensor_scalar(checks[:, 4:5], checks[:, 4:5], SPREAD, None, ALU.is_gt))
            after.link(nc.vector.tensor_tensor(checks[:, 5:6], checks[:, 2:3], checks[:, 3:4], ALU.max))
            nc.vector.tensor_tensor(checks[:, 0:1], checks[:, 5:6], checks[:, 4:5], ALU.max).then_inc(checks_ready, 1)
            dve.wait_ge(flag_ready, 1)
            needed = dve.value_load(flag[0:1, 0:1], min_val=0, max_val=1)
            with dve.If(needed != 0):
                general_vector(dve)
            dve.nop()


PACK_LINKS = 1 + (SLOTS // 8) + (SLOTS // 8 - 1) + GROUP_COLS + 1
LOGITS_LINKS = 2
FINISH_LINKS = 1
GENERAL_LINKS = 11


def diagonal(flat, start, step):
    ap = flat[:, start:start + BITS].rearrange("p (o t) -> p o t", o=1)
    dims = [list(d) for d in ap.ap]
    return bass.AP(tensor=ap.tensor, offset=ap.offset, ap=[dims[0], [step, PAIRS], [1, BITS]])


_INS = ["x", "adj", "L0_gnn_W1", "L0_gnn_b1", "L0_gnn_a1", "L0_gnn_a2", "L0_gnn_b2"]


def kernel(**inputs):
    import concourse.bacc as _bacc
    from concourse.bass_utils import run_bass_kernel_spmd as _run

    nc = _bacc.Bacc("TRN2", target_bir_lowering=False, num_devices=1)
    arrays, args = {}, []
    for name in _INS:
        a = np.ascontiguousarray(inputs[name])
        if a.ndim == 0:
            a = a.reshape(1, 1)
        arrays[name] = a
        args.append(nc.dram_tensor(name, a.shape, mybir.dt.from_np(a.dtype), kind="ExternalInput").ap())
    out = nc.dram_tensor("out", (N, D), F32, kind="ExternalOutput").ap()
    gat_kernel(nc, *args, out)
    return _run(nc, [arrays], core_ids=[0]).results[0]["out"]
```

```python
import numpy as np
import concourse.bass as bass
from concourse import mybir
from contextlib import ExitStack

F32, BF16, I32, I16 = mybir.dt.float32, mybir.dt.bfloat16, mybir.dt.int32, mybir.dt.int16
ALU = mybir.AluOpType
ACT = mybir.ActivationFunctionType
AX = mybir.AxisListType.X
RMAX = bass.bass_isa.ReduceOp.max

P = 128
N, D = 8192, 256
KD = D // P
BITS = 8
PACK_ROWS = P * BITS
PACKS = N // PACK_ROWS
TILES = N // P
TPP = TILES // PACKS
STEP_COLS = N // TPP
SUB = 512
SEGS = 8
SLOTS = P // 2
PAIRS = TPP
GROUP_COLS = 2
MIDDLE = ((1 << BITS) - 1) / 2
LOWEST = (1 - MIDDLE) * N - 0.5
TAKEN = -2.0 * MIDDLE * N
S2, ONE = D, D + 1
S1 = D + 1
ROW = D + 1
WIDE = D + 2
ALPHA = 0.2
EPS = 1e-5
MASKED = -1000000000000.0
SPREAD = 60.0
BATCH = 2
BATCHES = TILES // BATCH
BLOCK = 2
BLOCKS = BATCHES // BLOCK
X_RING = 4
H_RING = 8
RING = 4
HALVES = 2
UNITS = PACKS - 1 + HALVES
HALF_GROUPS = P // HALVES
HALF_BITS = BITS // HALVES
HALF_STEPS = (PACKS - 1) * TPP
HALF_TILES = TPP // HALVES
STEPS = UNITS * TPP
LAG = TPP + 1
WITHOUT_TILE = (2, 4, 6, 8, 11)
JB = 8


class Order:

    def __init__(self, eng, sem, passed, start=0):
        self.eng, self.sem, self.passed, self.n = eng, sem, passed, start

    def link(self, instruction, apart=False):
        instruction.then_inc(self.sem, 1)
        self.n = self.n + 1
        if apart:
            wait_apart(self.eng, self.sem, self.n, self.passed)
        else:
            self.eng.wait_ge(self.sem, self.n)


def wait_apart(eng, sem, value, passed):
    eng.wait_ge(sem, value)
    if not isinstance(value, int):
        eng.sem_inc(passed, 1)


def gat_kernel(nc, x, adj, W1, b1, a1, a2, b2, out):
    ctx = ExitStack()
    with ctx:
        def sb(name, shape, dt=F32):
            return ctx.enter_context(nc.sbuf_tensor(name, shape, dt))

        def sem(name):
            return ctx.enter_context(nc.semaphore(name))

        table = nc.dram_tensor("table", (N, ROW), F32, kind="Internal").ap()
        s1_dram = nc.dram_tensor("s1_dram", (GROUP_COLS, TILES, SLOTS), F32, kind="Internal").ap()
        s2_dram = nc.dram_tensor("s2_dram", (TILES, P), F32, kind="Internal").ap()

        adj_sb = sb("adj_sb", [P, 4, BITS, SUB], I32)
        signs = sb("signs", [P, 2, BITS, SUB], BF16)
        gathered = sb("gathered", [P, RING, PAIRS, WIDE])
        s1_half = sb("s1_half", [P, TILES, SLOTS])
        column = sb("column", [P, N], I16)
        key = sb("key", [P, 2, STEP_COLS])
        weights = sb("weights", [P, 2, PAIRS, P])
        row_bit = sb("row_bit", [P, 2, PAIRS, BITS], I32)
        bit_mask = sb("bit_mask", [P, BITS], I32)
        top8 = sb("top8", [P, 2, SEGS, 8])
        winners = sb("winners", [P, TPP, SEGS * 8])
        slots = sb("slots", [P, SLOTS])
        slots_twice = sb("slots_twice", [P, 2, SLOTS])
        words = sb("words", [P, PACKS, SLOTS], I32)
        absent = sb("absent", [P, SLOTS], I32)
        own_column = sb("own_column", [P, SLOTS], I32)
        index = sb("index", [P, PACKS, SLOTS], I32)
        index_now = sb("index_now", [P, RING, PAIRS], I32)
        logits = sb("logits", [P, 2, PAIRS * BITS])
        bound = sb("bound", [P, 2, PAIRS * BITS])
        exps = sb("exps", [P, 2, PAIRS * BITS])
        relu_out = sb("relu_out", [P, RING, D])
        exp_out = sb("exp_out", [P, RING, D])
        x_again = sb("x_again", [P, RING, D])
        result = sb("result", [P, RING, D])
        recip = sb("recip", [P, 2])
        density = sb("density", [P, TILES])
        full = sb("full", [P, 2, UNITS])
        normed = sb("normed", [P, BLOCK, BATCH, D])
        acts_t = sb("acts_t", [P, 2, KD, BATCH * P])
        stats = sb("stats", [P, 2, BLOCK * BATCH, 6])
        mean_var = sb("mean_var", [P, 2, BLOCK * BATCH, 2])
        std = sb("std", [P, 2, BLOCK * BATCH])
        rstd = sb("rstd", [P, 2, BLOCK * BATCH])
        w_ext = sb("w_ext", [P, KD + 1, WIDE])
        a_rows = sb("a_rows", [P, 2, D])
        b2_col = sb("b2_col", [P, 1])
        product = sb("product", [P, KD + 1, D])
        s_rows = sb("s_rows", [TILES, P])
        s_cols = sb("s_cols", [P, TILES, 2])
        ident = sb("ident", [P, P])
        scaled = sb("scaled", [P, BITS, P], BF16)
        scaled_half = sb("scaled_half", [P, HALF_BITS, HALF_GROUPS], BF16)
        eps_col = sb("eps_col", [P, 1])
        below = sb("below", [P, 1])
        zero_col = sb("zero_col", [P, 1])
        extremes = sb("extremes", [P, 2])
        bounds = sb("bounds", [P, 2])
        checks = sb("checks", [P, 8])
        flag_f = sb("flag_f", [P, 1])
        flag = sb("flag", [P, 1], I32)

        ps = ctx.enter_context(nc.psum_tensor("ps", [P, 8, SUB], F32))
        sums = [ps[:, 2 * q:2 * q + 2, :].rearrange("p k c -> p (k c)") for q in range(2)]
        slots_ps = ps[:, 6, 0:P]
        out_ps = [ps[:, 4 + q, 0:WIDE] for q in range(2)]
        h_ps = ps[:, 4:4 + BATCH, 0:WIDE]
        turned = ps[:, 6:8, :]
        s1_turned = ps[0:TILES, 7, 0:P]

        adj_in = [sem(f"adj_in{i}") for i in range(4)]
        signs_done = sem("signs_done")
        packs_done = sem("packs_done")
        sums_read = sem("sums_read")
        winners_kept = sem("winners_kept")
        slots_ready = sem("slots_ready")
        slots_turned = sem("slots_turned")
        index_ready = sem("index_ready")
        index_copied = sem("index_copied")
        rows_in = [sem(f"rows_in{i}") for i in range(RING)]
        logits_ready = sem("logits_ready")
        exps_ready = sem("exps_ready")
        weights_ready = sem("weights_ready")
        pv_done = sem("pv_done")
        recip_ready = sem("recip_ready")
        acts_done = sem("acts_done")
        x_again_in = [sem(f"x_again_in{i}") for i in range(RING)]
        result_ready = sem("result_ready")
        out_stored = [sem(f"out_stored{i}") for i in range(RING)]
        top8_order = sem("top8_order")
        pack_order = sem("pack_order")
        logits_order = sem("logits_order")
        bits_order = sem("bits_order")
        finish_order = sem("finish_order")
        x_in_sem = [sem(f"x_in{i}") for i in range(X_RING)]
        params_in = sem("params_in")
        ident_ready = sem("ident_ready")
        pool_consts = sem("pool_consts")
        scaled_ready = sem("scaled_ready")
        setup_order = sem("setup_order")
        stats_order = sem("stats_order")
        rstd_order = sem("rstd_order")
        rows_order = sem("rows_order")
        var_ready = sem("var_ready")
        std_ready = sem("std_ready")
        normed_ready = sem("normed_ready")
        s1_turned_ready = sem("s1_turned_ready")
        s1_rows_ready = sem("s1_rows_ready")
        s1_stored = sem("s1_stored")
        s1_in = sem("s1_in")
        turned_ready = sem("turned_ready")
        acts_t_ready = sem("acts_t_ready")
        h_ready = sem("h_ready")
        h_read = sem("h_read")
        table_stored = [sem(f"table_stored{i}") for i in range(H_RING)]
        extremes_ready = sem("extremes_ready")
        bounds_ready = sem("bounds_ready")
        attend_ready = sem("attend_ready")
        checks_ready = sem("checks_ready")
        checks_done = sem("checks_done")
        flag_ready = sem("flag_ready")
        passed = sem("passed")
        g_turn = sem("g_turn")
        g_s2 = sem("g_s2")
        g_s2_stored = sem("g_s2_stored")
        g_s2_in = sem("g_s2_in")
        g_order = sem("g_order")
        g_row_in = sem("g_row_in")
        g_scores = sem("g_scores")
        g_exps = sem("g_exps")
        g_h_in = sem("g_h_in")
        g_block = sem("g_block")
        g_block_ps = sem("g_block_ps")
        g_block_t = sem("g_block_t")
        g_part = sem("g_part")
        g_added = sem("g_added")
        g_low = sem("g_low")
        g_exp_out = sem("g_exp_out")
        g_result = sem("g_result")
        g_stored = sem("g_stored")

        bias_ext = w_ext[:, KD, :]

        adj_v = adj.rearrange("(b g t) (o s c) -> b o s g t c", g=P, t=BITS, s=2, c=SUB)
        half_v = adj[(PACKS - 1) * PACK_ROWS:, :].rearrange("(h g u t) (o c) -> h o u g t c", g=HALF_GROUPS, u=HALVES,
                                                            t=HALF_BITS, c=STEP_COLS)
        adj_half = adj_sb[:, :, :, :].rearrange("p i t c -> p i (t c)").rearrange("p i (t c) -> p i t c", c=STEP_COLS)
        signs_half = signs[:, :, :, :].rearrange("p i t c -> p i (t c)").rearrange("p i (t c) -> p i t c", c=STEP_COLS)
        x_block = x.rearrange("(m i p) f -> m p i f", i=BLOCK * BATCH, p=P)
        table_batch = table.rearrange("(m i p) f -> m p i f", i=BATCH, p=P)
        x_tile = x.rearrange("(k p) f -> k p f", p=P)
        out_tile = out.rearrange("(k p) f -> k p f", p=P)

        h_at = [0, BATCH + BLOCK * BATCH]
        h_sb = [gathered[:, q, at:at + BATCH, :] for at in h_at for q in range(RING)]
        x_in = [gathered[:, q, BATCH:BATCH + BLOCK * BATCH, 0:D] for q in range(X_RING)]

        flat = adj_sb[:, :, :, :].rearrange("p a t c -> p (a t c)")
        g_row, g_rowf = flat[:, 0:N], flat[:, 0:N].bitcast(F32)
        g_e = flat[:, N:2 * N].bitcast(F32)
        g_s2b = gathered[:, :, :, :].rearrange("p a t c -> p (a t c)")[:, 0:N]
        g_h = s1_half[:, :, :].rearrange("p t c -> p (t c)")[:, 0:JB * D].rearrange("p (j f) -> p j f", j=JB)
        g_blk, g_blk_t = weights[:, 0, 0, :], weights[:, 0, 1, :]
        g_acc = weights[:, 1, 0:2, :].rearrange("p a c -> p (a c)")
        table_jb = table.rearrange("(b j p) f -> b p j f", j=JB, p=P)

        block = ctx.enter_context(nc.Block())

        def general_loads(sp):
            sp.wait_ge(g_s2, 1)
            sp.dma_start(s2_dram, s_rows[:, :]).then_inc(g_s2_stored, 16)
            sp.wait_ge(g_s2_stored, 16)
            sp.dma_start(g_s2b, s2_dram.rearrange("(o i) p -> o (i p)", o=1).broadcast_to([P, N])).then_inc(g_s2_in, 16)
            with sp.Fori(0, TILES) as i:
                wait_apart(sp, g_scores, i + 1, passed)
                wait_apart(sp, g_stored, 16 * i + 16, passed)
                sp.dma_start(g_row, adj.rearrange("(i p) n -> i p n", p=P)[i]).then_inc(g_row_in, 16)
                sp.dma_start(x_again[:, 0, :], x_tile[i]).then_inc(g_row_in, 16)
                with sp.Fori(0, TILES // JB) as jb:
                    wait_apart(sp, g_part, i * TILES + jb * JB + 1, passed)
                    sp.dma_start(g_h, table_jb[jb][:, :, 0:D]).then_inc(g_h_in, 16)
                wait_apart(sp, g_result, i + 1, passed)
                sp.dma_start(out_tile[i], result[:, 0, :]).then_inc(g_stored, 16)
            wait_apart(sp, g_stored, 16 * TILES + 16, passed)

        def general_scalar(act):
            with act.Fori(0, TILES) as i:
                act.wait_ge(g_scores, i + 2)
                nc.scalar.activation(g_e, g_e, ACT.Exp, bias=checks[:, 1:2], accum_out=checks[:, 2:3]).then_inc(g_exps, 1)
                act.wait_ge(g_low, i + 1)
                nc.scalar.activation(exp_out[:, 0, :], exp_out[:, 0, :], ACT.Exp, bias=zero_col[:, :]).then_inc(g_exp_out, 1)

        def general_tensor(pe):
            nc.tensor.transpose(ps[0:TILES, 0, 0:P], s_cols[:, :, 0], ident[:, :]).then_inc(g_turn, 1)
            with pe.Fori(0, TILES) as i:
                with pe.Fori(0, TILES // JB) as jb:
                    for jj in range(JB):
                        u = i * TILES + jb * JB + jj
                        pe.wait_ge(g_block, u + 1)
                        nc.tensor.transpose(ps[:, 1, 0:P], g_blk, ident[:, :]).then_inc(g_block_ps, 1)
                        pe.wait_ge(g_block_t, u + 1)
                        pe.wait_ge(g_h_in, 16 * (i * (TILES // JB) + jb + 1))
                        nc.tensor.matmul(ps[:, 2, 0:D], g_blk_t, g_h[:, jj, :], start=True, stop=True).then_inc(g_part, 1)

        def general_vector(dve):
            dve.sem_inc(g_scores, 1)
            dve.sem_inc(g_stored, 16)
            dve.sem_inc(g_part, 1)
            dve.wait_ge(g_turn, 1)
            nc.vector.tensor_copy(s_rows[:, :], ps[0:TILES, 0, 0:P]).then_inc(g_s2, 1)
            dve.wait_ge(g_s2_in, 16)
            with dve.Fori(0, TILES) as i:
                order = Order(dve, g_order, passed, i * GENERAL_LINKS)
                dve.wait_ge(g_row_in, 32 * i + 32)
                dve.wait_ge(g_part, i * TILES + 1)
                order.link(nc.vector.tensor_copy(checks[:, 0:1], s_cols[:, bass.ds(i, 1), 1]))
                order.link(nc.vector.tensor_scalar(g_e, g_s2b, checks[:, 0:1], None, ALU.add))
                order.link(nc.vector.scalar_tensor_tensor(g_e, g_e, ALPHA, g_e, ALU.mult, ALU.max))
                order.link(nc.vector.scalar_tensor_tensor(g_e, g_row, 0.0, g_e, ALU.is_gt, ALU.mult))
                order.link(nc.vector.tensor_scalar(g_rowf, g_row, 0.0, MASKED, ALU.is_le, ALU.mult))
                order.link(nc.vector.tensor_tensor(g_e, g_e, g_rowf, ALU.add))
                order.link(nc.vector.reduce_max(checks[:, 3:4], g_e, AX))
                order.link(nc.vector.memset(g_acc, 0.0))
                nc.vector.tensor_scalar(checks[:, 1:2], checks[:, 3:4], -1.0, None, ALU.mult).then_inc(g_scores, 1)
                wait_apart(dve, g_exps, i + 1, passed)
                order.link(nc.vector.reciprocal(checks[:, 4:5], checks[:, 2:3]), apart=True)
                with dve.Fori(0, TILES // JB) as jb:
                    for jj in range(JB):
                        u = i * TILES + jb * JB + jj
                        nc.vector.tensor_copy(g_blk, g_e[:, bass.ds((jb * JB + jj) * P, P)]).then_inc(g_block, 1)
                        dve.wait_ge(g_block_ps, u + 1)
                        nc.vector.tensor_copy(g_blk_t, ps[:, 1, 0:P]).then_inc(g_block_t, 1)
                        dve.wait_ge(g_part, u + 2)
                        nc.vector.tensor_tensor(g_acc, g_acc, ps[:, 2, 0:D], ALU.add).then_inc(g_added, 1)
                        dve.wait_ge(g_added, u + 1)
                dve.wait_ge(g_stored, 16 * i + 16)
                order.link(nc.vector.tensor_scalar(relu_out[:, 0, :], g_acc, checks[:, 4:5], 0.0, ALU.mult, ALU.max))
                nc.vector.tensor_scalar(exp_out[:, 0, :], g_acc, checks[:, 4:5], 0.0, ALU.mult, ALU.min).then_inc(g_low, 1)
                dve.wait_ge(g_exp_out, i + 1)
                order.link(nc.vector.scalar_tensor_tensor(exp_out[:, 0, :], exp_out[:, 0, :], -1.0, relu_out[:, 0, :],
                                                          ALU.add, ALU.add))
                nc.vector.tensor_tensor(result[:, 0, :], exp_out[:, 0, :], x_again[:, 0, :], ALU.add).then_inc(g_result, 1)

        def is_first_pack(b):
            return isinstance(b, int) and b == 0

        def is_half(b):
            return isinstance(b, int) and b >= PACKS - 1

        def loads(k, b):
            return k + HALF_STEPS if is_half(b) else 2 * k

        def lanes(b):
            return slice(0, HALF_GROUPS if is_half(b) else P)

        def tile_at(k, b, i, later=0):
            if not isinstance(k, int) or k - later < HALF_STEPS:
                t = k - later - LAG
                return t, (i - later - LAG) % RING, not isinstance(k, int) or t >= 0
            j = k - later - HALF_STEPS
            t = HALF_STEPS - LAG + j - sum(w < j for w in WITHOUT_TILE)
            return t, t % RING, t < TILES and j not in WITHOUT_TILE

        def all_steps(eng, step, unit_end):
            def body(k, b, o):
                for i in range(RING):
                    step(k + i, b, o + i, i)

            def unrolled(b):
                for g in range(TPP // RING):
                    body(b * TPP + g * RING, b, g * RING)
                unit_end(b)

            unrolled(0)
            unrolled(1)
            with eng.Fori(2, PACKS - 1) as b:
                with eng.Fori(0, TPP // RING) as g:
                    body(b * TPP + g * RING, b, g * RING)
                unit_end(b)
            for b in range(PACKS - 1, UNITS):
                unrolled(b)
            for i in range(TILES - HALF_STEPS + LAG + len(WITHOUT_TILE) + 5 - HALVES * TPP):
                step(STEPS + i, None, None, i % RING)

        def ring_value(t, i, per_use, ring=RING, uses=1):
            return (t - i) * (per_use // ring) + uses * per_use

        @block.sync
        def _(sp):
            sp.dma_start(w_ext[:, 0:KD, 0:D], W1.rearrange("(k p) f -> p k f", p=P)).then_inc(params_in, 16)
            sp.dma_start(a_rows[:, 0, :], a1.rearrange("(o f) -> o f", o=1).broadcast_to([P, D])).then_inc(params_in, 16)
            sp.dma_start(a_rows[:, 1, :], a2.rearrange("(o f) -> o f", o=1).broadcast_to([P, D])).then_inc(params_in, 16)
            sp.dma_start(w_ext[:, KD, 0:D], b1.rearrange("(o f) -> o f", o=1).broadcast_to([P, D])).then_inc(params_in, 16)
            sp.dma_start(b2_col[:, :], b2.broadcast_to([P, 1])).then_inc(params_in, 16)

            with sp.Fori(0, PACKS - 1) as b:
                with sp.Fori(0, TPP // 2) as j:
                    for p in range(2):
                        for s in range(2):
                            i = 2 * p + s
                            wait_apart(sp, signs_done, b * 16 + 4 * j + i + 1, passed)
                            sp.dma_start(adj_sb[:, i, :, :], adj_v[b, 2 * j + p, s]).then_inc(adj_in[i], 16)
            with sp.Fori(0, HALVES) as h:
                with sp.Fori(0, TPP // RING) as j:
                    for i in range(RING):
                        wait_apart(sp, signs_done, h * TPP + j * RING + 2 * HALF_STEPS + i + 1, passed)
                        for u in range(HALVES):
                            sp.dma_start(adj_half[u * HALF_GROUPS:(u + 1) * HALF_GROUPS, i, :, :],
                                         half_v[h, j * RING + i, u]).then_inc(adj_in[i], 16)

            sp.wait_ge(flag_ready, 1)
            needed = sp.value_load(flag[0:1, 0:1], min_val=0, max_val=1)
            with sp.If(needed != 0):
                general_loads(sp)
            sp.nop()

        @block.gpsimd
        def _(pool):
            pool.memset(ident[:, :], 0.0).then_inc(ident_ready, 1)
            pool.wait_ge(ident_ready, 1)
            pool.affine_select(out=ident[:, :], in_=ident[:, :], compare_op=ALU.not_equal, fill=1.0, base=0,
                               pattern=[[-1, P]], channel_multiplier=1).then_inc(ident_ready, 1)
            pool.iota(column[:, :], pattern=[[1, N]], base=0, channel_multiplier=0).then_inc(pool_consts, 1)
            pool.memset(weights[:, :, :, :], 0.0).then_inc(pool_consts, 1)
            x_rows = slice(BATCH, BATCH + BLOCK * BATCH)
            pool.memset(gathered[:, :, x_rows, S2:S2 + 1], -1e30)
            pool.memset(gathered[:, :, x_rows, ONE:ONE + 1], 1.0).then_inc(pool_consts, 1)
            with pool.Fori(0, BATCHES // H_RING) as m:
                for q in range(H_RING):
                    wait_apart(pool, h_read, H_RING * m + q + 1, passed)
                    pool.dma_start(table_batch[H_RING * m + q], h_sb[q][:, :, 0:ROW]).then_inc(table_stored[q], 16)
            pool.wait_ge(extremes_ready, 1)
            pool.partition_all_reduce(bounds[:, :], extremes[:, :], P, RMAX).then_inc(bounds_ready, 1)
            pool.wait_ge(s1_rows_ready, 1)
            for g in range(GROUP_COLS):
                pool.dma_start(s1_dram[g].rearrange("t (i b) -> t i b", b=BITS),
                               s_rows[:, :].rearrange("t (i g b) -> t i g b", g=GROUP_COLS, b=BITS)[:, :, g, :])\
                    .then_inc(s1_stored, 16)
            pool.wait_ge(s1_stored, 32)
            for g in range(GROUP_COLS):
                pool.dma_start(s1_half[g * SLOTS:(g + 1) * SLOTS, :, :].rearrange("p t c -> p (t c)"),
                               s1_dram[g].rearrange("(o t) c -> o (t c)", o=1).broadcast_to([SLOTS, TILES * SLOTS]))\
                    .then_inc(s1_in, 16)
            for q in range(H_RING):
                pool.wait_ge(table_stored[q], 16 * (BATCHES // H_RING))
            pool.wait_ge(attend_ready, 1)

            def gather_tiles(b, t, first):
                for i in range(RING):
                    pool.wait_ge(pv_done, t + i + 1)
                    pool.tensor_copy(index_now[:, i, :], index[:, b, bass.ds((first + i) * PAIRS, PAIRS)])\
                        .then_inc(index_copied, 1)
                    wait_apart(pool, index_copied, t + i + 1, passed)
                    for q in range(PAIRS):
                        pool.indirect_dma_start(
                            out=gathered[:, i, q, 0:ROW], out_offset=None, in_=table,
                            in_offset=bass.IndirectOffsetOnAxis(ap=index_now[:, i, q:q + 1], axis=0),
                            bounds_check=N - 1, oob_is_err=False).then_inc(rows_in[i], 16)

            with pool.Fori(0, PACKS - 1) as b:
                wait_apart(pool, index_ready, b + 1, passed)
                with pool.Fori(0, TPP // RING) as g:
                    gather_tiles(b, b * TPP + g * RING, g * RING)
            for h in range(HALVES):
                pool.wait_ge(index_ready, PACKS + h)
                gather_tiles(PACKS - 1, TILES - TPP + h * HALF_TILES, h * HALF_TILES)
            pool.wait_ge(checks_ready, 1)
            pool.partition_all_reduce(flag_f[:, :], checks[:, 0:1], P, RMAX).then_inc(checks_done, 1)
            pool.wait_ge(checks_done, 1)
            pool.tensor_copy(flag[:, :], flag_f[:, :]).then_inc(flag_ready, 1)

        @block.scalar
        def _(act):
            act.sem_inc(acts_done, 2)
            act.sem_inc(signs_done, 4)

            def take_signs_half(k, p, i):
                act.wait_ge(adj_in[i], ring_value(k - HALF_STEPS, i, 32) + HALF_STEPS // 2 * 16)
                act.wait_ge(packs_done, k + HALF_STEPS + 1)
                nc.scalar.activation(signs_half[:, p, :, :], adj_half[:, i, :, :], ACT.Sign,
                                     bias=below[:, :]).then_inc(signs_done, 1)

            def load_x(m):
                if m >= X_RING:
                    act.wait_ge(normed_ready, (m - X_RING + 1) * BLOCK)
                act.dma_start(x_in[m % X_RING], x_block[m]).then_inc(x_in_sem[m % X_RING], 16)

            def take_signs(k, p, s):
                i = 2 * p + s
                act.wait_ge(adj_in[i], ring_value(k, p, 16, 2))
                act.wait_ge(packs_done, 2 * k + s + 1)
                nc.scalar.activation(signs[:, s, :, :], adj_sb[:, i, :, :], ACT.Sign,
                                     bias=below[:, :]).then_inc(signs_done, 1)

            def rectify(u):
                q = u % 2
                act.wait_ge(turned_ready, u + 1)
                if u >= 2:
                    act.wait_ge(h_ready, u - 1)
                nc.scalar.activation(acts_t[:, q, :, :].rearrange("p k c -> p (k c)"), turned[:, q, :], ACT.Relu)\
                    .then_inc(acts_t_ready, 1)

            def deviations(m):
                act.wait_ge(var_ready, m + 1)
                nc.scalar.activation(std[:, m % 2, :], mean_var[:, m % 2, :, 1], ACT.Sqrt, bias=eps_col[:, :])\
                    .then_inc(std_ready, 1)

            def half_step(m):
                if m + X_RING < BLOCKS:
                    load_x(m + X_RING)
                for n in range(BLOCK):
                    rectify(m * BLOCK + n)
                if m + 2 < BLOCKS:
                    deviations(m + 2)

            def step(k, b, o, i):
                p = i % 2
                if is_half(b):
                    take_signs_half(k, p, i)
                elif b is not None:
                    take_signs(k, p, 0)
                if is_first_pack(b):
                    half_step(2 * k)
                t, ring, real = tile_at(k, b, i, 1)
                if real:
                    exponents(t, ring % 2)
                if b is not None and not is_half(b):
                    take_signs(k, p, 1)
                if is_first_pack(b):
                    half_step(2 * k + 1)
                t, ring, real = tile_at(k, b, i, 2)
                if real:
                    fetch_x(t, ring)
                    normalise(t, ring % 2, ring)
                t, ring, real = tile_at(k, b, i, 5)
                if real:
                    store(t, ring)

            def fetch_x(t, q):
                act.wait_ge(result_ready, t + 1)
                act.dma_start(x_again[:, q, :], x_tile[t]).then_inc(x_again_in[q], 16)

            def exponents(t, q):
                act.wait_ge(logits_ready, t + 1)
                nc.scalar.activation(exps[:, q, :], logits[:, q, :], ACT.Exp, bias=zero_col[:, :]).then_inc(exps_ready, 1)

            def normalise(t, q, ring):
                act.wait_ge(recip_ready, t + 1)
                nc.scalar.activation(relu_out[:, ring, :], out_ps[q][:, 0:D], ACT.Relu, scale=recip[:, q:q + 1])
                nc.scalar.activation(exp_out[:, ring, :], out_ps[q][:, 0:D], ACT.Exp, bias=zero_col[:, :],
                                     scale=recip[:, q:q + 1]).then_inc(acts_done, 1)

            def store(t, q):
                act.wait_ge(result_ready, t + RING + 1)
                act.dma_start(out_tile[t], result[:, q, :]).then_inc(out_stored[q], 16)

            for m in range(X_RING):
                load_x(m)
            for m in range(2):
                deviations(m)
            all_steps(act, step, lambda b: None)
            for p in range(RING):
                act.wait_ge(out_stored[p], 16 * (TILES // RING) + 16)
            act.wait_ge(flag_ready, 1)
            needed = act.value_load(flag[0:1, 0:1], min_val=0, max_val=1)
            with act.If(needed != 0):
                general_scalar(act)
            act.nop()

        @block.tensor
        def _(pe):
            pe.sem_inc(packs_done, 2)
            pe.sem_inc(pv_done, RING)
            pe.wait_ge(ident_ready, 2)
            pe.wait_ge(scaled_ready, BITS + 2)

            def turn(u):
                q = u % 2
                pe.wait_ge(normed_ready, u + 1)
                if u >= 2:
                    pe.wait_ge(acts_t_ready, u - 1)
                for k in range(KD):
                    for i in range(BATCH):
                        last = nc.tensor.transpose(turned[:, q, (k * BATCH + i) * P:(k * BATCH + i + 1) * P],
                                                   normed[:, u % BLOCK, i, k * P:(k + 1) * P], ident[:, :])
                last.then_inc(turned_ready, 1)

            def project(u):
                q = u % 2
                pe.wait_ge(acts_t_ready, u + 1)
                if u >= 1:
                    pe.wait_ge(h_read, u)
                for i in range(BATCH):
                    for k in range(KD):
                        last = nc.tensor.matmul(h_ps[:, i, :], acts_t[:, q, k, i * P:(i + 1) * P], w_ext[:, k, :],
                                                start=(k == 0), stop=(k == KD - 1))
                last.then_inc(h_ready, 1)

            def half_step(m):
                for n in range(BLOCK):
                    project(m * BLOCK + n)
                    if m + 1 < BLOCKS:
                        turn((m + 1) * BLOCK + n)

            def add_signs(k, p, s):
                if s == 0:
                    pe.wait_ge(sums_read, k + 1)
                pe.wait_ge(signs_done, 2 * k + s + 5)
                for t in range(BITS):
                    last = nc.tensor.matmul(sums[p][:, s * SUB:(s + 1) * SUB], scaled[:, t, :], signs[:, s, t, :],
                                            start=(t == 0), stop=(t == BITS - 1))
                last.then_inc(packs_done, 1)

            def add_signs_half(k, p):
                pe.wait_ge(sums_read, k + 1)
                pe.wait_ge(signs_done, k + HALF_STEPS + 5)
                for s in range(2):
                    cols = slice(s * SUB, (s + 1) * SUB)
                    for t in range(HALF_BITS):
                        last = nc.tensor.matmul(sums[p][0:HALF_GROUPS, cols], scaled_half[:, t, :],
                                                signs_half[:, p, t, cols], start=(t == 0), stop=(t == HALF_BITS - 1))
                last.then_inc(packs_done, 1)

            def turn_slots(b):
                pe.wait_ge(slots_ready, b + 1)
                n = lanes(b)
                nc.tensor.transpose(slots_ps[:, n], slots_twice[n, :, :].rearrange("p a c -> p (a c)"), ident[n, n])\
                    .then_inc(slots_turned, 1)

            def weigh(t, q, ring):
                pe.wait_ge(weights_ready, 2 * t + 2)
                pe.wait_ge(acts_done, t + 1)
                for i in range(PAIRS):
                    last = nc.tensor.matmul(out_ps[q], weights[:, q, i, :], gathered[:, ring, i, :],
                                            start=(i == 0), stop=(i == PAIRS - 1))
                last.then_inc(pv_done, 1)

            def step(k, b, o, i):
                if is_half(b):
                    add_signs_half(k, i % 2)
                elif b is not None:
                    for s in range(2):
                        add_signs(k, i % 2, s)
                        if is_first_pack(b):
                            half_step(2 * k + s)
                t, ring, real = tile_at(k, b, i, 1)
                if real:
                    weigh(t, ring % 2, ring)

            def unit_end(b):
                if is_first_pack(b):
                    pe.wait_ge(h_read, BATCHES)
                    nc.tensor.transpose(s1_turned, s_cols[:, :, 1], ident[:, :]).then_inc(s1_turned_ready, 1)
                turn_slots(b)

            for u in range(BLOCK):
                turn(u)
            all_steps(pe, step, unit_end)
            pe.wait_ge(flag_ready, 1)
            needed = pe.value_load(flag[0:1, 0:1], min_val=0, max_val=1)
            with pe.If(needed != 0):
                general_tensor(pe)
            pe.nop()

        @block.vector
        def _(dve):
            for q in range(RING):
                dve.sem_inc(out_stored[q], 16)
            dve.sem_inc(sums_read, 2)
            dve.sem_inc(result_ready, RING)
            nc.vector.memset(eps_col[:, :], EPS)
            nc.vector.memset(below[:, :], -0.5)
            nc.vector.memset(zero_col[:, :], 0.0)
            for t in range(BITS):
                nc.vector.memset(bit_mask[:, t:t + 1], N << t)
            dve.wait_ge(ident_ready, 2)
            for t in range(BITS):
                nc.vector.tensor_scalar(scaled[:, t, :], ident[:, :], (1 << t) / 2, None, ALU.mult)\
                    .then_inc(scaled_ready, 1)
            dve.wait_ge(scaled_ready, BITS)
            for u in range(HALVES):
                rows = slice(u * HALF_GROUPS, (u + 1) * HALF_GROUPS)
                nc.vector.tensor_copy(scaled_half[rows, :, :], scaled[rows, u * HALF_BITS:(u + 1) * HALF_BITS, rows])\
                    .then_inc(scaled_ready, 1)
            nc.vector.memset(full[:, :, :], TAKEN)
            dve.wait_ge(params_in, 80)
            setup = Order(dve, setup_order, passed)
            for c, a in ((S2, 1), (S1, 0)):
                setup.link(nc.vector.tensor_tensor(
                    product[:, :, :], w_ext[:, :, 0:D],
                    a_rows[:, a, :].rearrange("p (o f) -> p o f", o=1).broadcast_to([P, KD + 1, D]), ALU.mult))
                setup.link(nc.vector.reduce_sum(w_ext[:, :, c], product[:, :, :], AX))
            setup.link(nc.vector.tensor_tensor(bias_ext[:, S1:S1 + 1], bias_ext[:, S1:S1 + 1], b2_col[:, :], ALU.add))

            def take_stats(m):
                dve.wait_ge(x_in_sem[m % X_RING], 16 * (m // X_RING) + 16)
                for i in range(BLOCK * BATCH):
                    last = nc.vector.bn_stats(stats[:, m % 2, i, :], x_in[m % X_RING][:, i, :])
                last.then_inc(stats_order, 1)
                wait_apart(dve, stats_order, m + 1, passed)
                for i in range(BLOCK * BATCH):
                    last = nc.vector.bn_aggr(mean_var[:, m % 2, i, :], stats[:, m % 2, i, :])
                last.then_inc(var_ready, 1)

            def norm(m):
                dve.wait_ge(std_ready, m + 1)
                nc.vector.reciprocal(rstd[:, m % 2, :], std[:, m % 2, :]).then_inc(rstd_order, 1)
                dve.wait_ge(rstd_order, m + 1)
                for n in range(BLOCK):
                    if m > 0:
                        dve.wait_ge(turned_ready, (m - 1) * BLOCK + n + 1)
                    for i in range(BATCH):
                        j = n * BATCH + i
                        last = nc.vector.tensor_scalar(normed[:, n, i, :], x_in[m % X_RING][:, j, :],
                                                       mean_var[:, m % 2, j, 0:1], rstd[:, m % 2, j:j + 1],
                                                       ALU.subtract, ALU.mult)
                    last.then_inc(normed_ready, 1)

            def take_rows(u):
                ring = u % H_RING
                dve.wait_ge(h_ready, u + 1)
                if u >= H_RING:
                    dve.wait_ge(table_stored[ring], 16 * (u // H_RING))
                nc.vector.tensor_tensor(
                    h_sb[ring], h_ps, bias_ext.rearrange("p (o f) -> p o f", o=1).broadcast_to([P, BATCH, WIDE]),
                    ALU.add).then_inc(rows_order, 1)
                dve.wait_ge(rows_order, u + 1)
                nc.vector.tensor_copy(s_cols[:, u * BATCH:(u + 1) * BATCH, :], h_sb[ring][:, :, S2:S2 + 2])\
                    .then_inc(h_read, 1)

            def half_step(m):
                take_rows(m * BLOCK)
                if m + 3 < BLOCKS:
                    take_stats(m + 3)
                take_rows(m * BLOCK + 1)
                if m + 2 < BLOCKS:
                    norm(m + 2)
                if m % 2 == 0 and m > 0:
                    take_top(m // 2 - 1, 0, (m // 2 - 1) % 2)
                    keep_winners(m // 2 - 1, 0, m // 2 - 1, (m // 2 - 1) % 2)

            def end_projection():
                dve.wait_ge(h_read, BATCHES)
                setup.link(nc.vector.reduce_max(extremes[:, 0:1], s_cols[:, :, 0], AX))
                setup.link(nc.vector.tensor_reduce(checks[:, 1:2], s_cols[:, :, 0], AX, ALU.min))
                nc.vector.tensor_scalar(extremes[:, 1:2], checks[:, 1:2], -1.0, None, ALU.mult).then_inc(extremes_ready, 1)
                dve.wait_ge(s1_turned_ready, 1)
                nc.vector.tensor_copy(s_rows[:, :], s1_turned).then_inc(s1_rows_ready, 1)

            def begin_tiles():
                for q in range(H_RING):
                    dve.wait_ge(table_stored[q], 16 * (BATCHES // H_RING))
                for at in h_at:
                    last = nc.vector.memset(gathered[:, :, at:at + BATCH, ONE:ONE + 1], 1.0)
                last.then_inc(attend_ready, 1)
                dve.wait_ge(bounds_ready, 1)
                dve.wait_ge(s1_in, 16 * GROUP_COLS)

            def make_keys(k, b, o, p):
                n = lanes(b)
                dve.wait_ge(packs_done, loads(k + 1, b) + 2)
                nc.vector.scalar_tensor_tensor(key[n, p, :], sums[p][n, :], float(N),
                                               column[n, bass.ds(o * STEP_COLS, STEP_COLS)],
                                               ALU.mult, ALU.add).then_inc(sums_read, 1)

            def take_top(k, b, p):
                n = lanes(b)
                wait_apart(dve, sums_read, k + 3, passed)
                by_seg = key[n, p, :].rearrange("p (c s) -> p s c", s=SEGS)
                for s in range(SEGS):
                    last = nc.vector.max(top8[n, p, s, :], by_seg[:, s, :])
                last.then_inc(top8_order, 1)

            def keep_winners(k, b, o, p):
                n = lanes(b)
                dve.wait_ge(top8_order, k + 1)
                nc.vector.tensor_copy(winners[n, bass.ds(o, 1), :].rearrange("p o c -> p (o c)"),
                                      top8[n, p, :, :].rearrange("p s c -> p (s c)")).then_inc(winners_kept, 1)

            def list_pack(b):
                n = lanes(b)
                order = Order(dve, pack_order, passed, b * PACK_LINKS)
                flat_w = winners[n, :, :].rearrange("p o c -> p (o c)")
                top = slots[n, :]
                dve.wait_ge(winners_kept, TPP * b + TPP)
                order.link(nc.vector.reduce_max(full[n, 0, bass.ds(b, 1)],
                                                flat_w.rearrange("p (n e) -> p n e", e=8)[:, :, 7], AX), apart=True)
                for r in range(SLOTS // 8):
                    order.link(nc.vector.max(top[:, 8 * r:8 * r + 8], flat_w), apart=True)
                    if r < SLOTS // 8 - 1:
                        order.link(nc.vector.match_replace(flat_w, top[:, 8 * r:8 * r + 8], flat_w, TAKEN), apart=True)
                nc.vector.tensor_copy(full[n, 1, bass.ds(b, 1)], top[:, SLOTS - 1:SLOTS])
                nc.vector.tensor_scalar(
                    slots_twice[n, :, :], top.rearrange("p (o c) -> p o c", o=1).broadcast_to([n.stop, 2, SLOTS]),
                    MIDDLE * N, None, ALU.add).then_inc(slots_ready, 1)
                dve.wait_ge(slots_turned, b + 1)
                pack = b
                pairs = slice(0, SLOTS)
                if is_half(b):
                    pack = PACKS - 1
                    pairs = slice((b - pack) * SLOTS // HALVES, (b - pack + 1) * SLOTS // HALVES)
                for g in range(GROUP_COLS):
                    rows = slice(g * SLOTS, (g + 1) * SLOTS)
                    order.link(nc.vector.tensor_copy(words[rows, pack, pairs],
                                                     slots_ps[rows, n].rearrange("p (n g) -> p n g", g=GROUP_COLS)[:, :, g]))
                nc.vector.tensor_scalar(absent[:, pairs], words[:, pack, pairs], float(N), float(N), ALU.is_lt, ALU.mult)
                order.link(nc.vector.tensor_scalar(own_column[:, pairs], words[:, pack, pairs], N - 1, None,
                                                   ALU.bitwise_and))
                nc.vector.tensor_tensor(index[:, pack, pairs], absent[:, pairs], own_column[:, pairs], ALU.bitwise_or)\
                    .then_inc(index_ready, 1)

            words_by_tile = words[:, :, :].rearrange("p b (i q) -> p (b i) q", q=PAIRS)

            def make_logits(t, q, ring):
                order = Order(dve, logits_order, passed, t * LOGITS_LINKS)
                lg, bd, s1 = logits[:, q, :], bound[:, q, :], s1_half[:, bass.ds(t, 1), :]
                order.link(nc.vector.tensor_scalar(bd, s1.rearrange("p o c -> p (o c)"), bounds[:, 0:1], None, ALU.add))
                order.link(nc.vector.scalar_tensor_tensor(bd, bd, ALPHA, bd, ALU.mult, ALU.max))
                dve.wait_ge(rows_in[ring], ring_value(t, ring, 16 * PAIRS))
                order.link(nc.vector.tensor_tensor(
                    lg.rearrange("p (i t) -> p i t", t=BITS),
                    s1.rearrange("p o (i t) -> p (o i) t", t=BITS),
                    gathered[:, ring, :, S2:S2 + 1].broadcast_to([P, PAIRS, BITS]), ALU.add))
                order.link(nc.vector.scalar_tensor_tensor(lg, lg, ALPHA, lg, ALU.mult, ALU.max))
                nc.vector.tensor_tensor(lg, lg, bd, ALU.subtract).then_inc(logits_ready, 1)
                nc.vector.tensor_tensor(
                    row_bit[:, q, :, :],
                    words_by_tile[:, bass.ds(t, 1), :].rearrange("p o i -> p (o i)").rearrange("p (i o) -> p i o", o=1)
                    .broadcast_to([P, PAIRS, BITS]),
                    bit_mask[:, :].rearrange("p (o t) -> p o t", o=1).broadcast_to([P, PAIRS, BITS]),
                    ALU.bitwise_and).then_inc(bits_order, 1)

            def make_weights(t, q):
                dve.wait_ge(exps_ready, t + 1)
                dve.wait_ge(bits_order, t + 1)
                dve.wait_ge(pv_done, t + RING - 1)
                for g in range(GROUP_COLS):
                    rows = slice(g * SLOTS, (g + 1) * SLOTS)
                    nc.vector.scalar_tensor_tensor(
                        diagonal(weights[rows, q, :, :].rearrange("p i c -> p (i c)"), g * BITS, P + GROUP_COLS * BITS),
                        row_bit[rows, q, :, :], 0.0,
                        exps[rows, q, :].rearrange("p (i t) -> p i t", t=BITS), ALU.is_gt, ALU.mult)\
                        .then_inc(weights_ready, 1)

            def invert(t, q):
                dve.wait_ge(pv_done, t + RING + 1)
                nc.vector.tensor_copy(density[:, bass.ds(t, 1)], out_ps[q][:, ONE:ONE + 1])
                nc.vector.reciprocal(recip[:, q:q + 1], out_ps[q][:, ONE:ONE + 1]).then_inc(recip_ready, 1)

            def finish(t, q):
                order = Order(dve, finish_order, passed, t * FINISH_LINKS)
                dve.wait_ge(acts_done, t + 3)
                dve.wait_ge(x_again_in[q], ring_value(t, q, 16))
                dve.wait_ge(out_stored[q], ring_value(t, q, 16))
                nc.vector.tensor_scalar(exp_out[:, q, :], exp_out[:, q, :], 1.0, -1.0, ALU.min, ALU.add)
                order.link(nc.vector.tensor_tensor(relu_out[:, q, :], relu_out[:, q, :], x_again[:, q, :], ALU.add))
                nc.vector.tensor_tensor(result[:, q, :], relu_out[:, q, :], exp_out[:, q, :], ALU.add)\
                    .then_inc(result_ready, 1)

            def step(k, b, o, i):
                p = i % 2
                t, ring, real = tile_at(k, b, i)
                if real:
                    make_logits(t, ring % 2, ring)
                if is_first_pack(b):
                    for n in range(2):
                        half_step(2 * k + n)
                if b is not None:
                    make_keys(k, b, o, p)
                    if not is_first_pack(b) or k == TPP - 1:
                        take_top(k, b, p)
                t3, ring3, real3 = tile_at(k, b, i, 3)
                if real3:
                    finish(t3, ring3)
                t1, ring1, real1 = tile_at(k, b, i, 1)
                if real1:
                    invert(t1, ring1 % 2)
                if real:
                    make_weights(t, ring % 2)
                if b is not None and (not is_first_pack(b) or k == TPP - 1):
                    keep_winners(k, b, o, p)

            def unit_end(b):
                if is_first_pack(b):
                    end_projection()
                list_pack(b)
                if is_first_pack(b):
                    begin_tiles()

            take_stats(0)
            take_stats(1)
            norm(0)
            take_stats(2)
            norm(1)
            dve.wait_ge(pool_consts, 3)
            all_steps(dve, step, unit_end)

            after = Order(dve, setup_order, passed, setup.n)
            after.link(nc.vector.reduce_max(checks[:, 2:3], full[:, :, :].rearrange("p a b -> p (a b)"), AX))
            after.link(nc.vector.tensor_scalar(checks[:, 2:3], checks[:, 2:3], LOWEST, None, ALU.is_gt))
            after.link(nc.vector.tensor_reduce(checks[:, 3:4], density[:, :], AX, ALU.min))
            after.link(nc.vector.tensor_scalar(checks[:, 3:4], checks[:, 3:4], 0.0, None, ALU.is_le))
            after.link(nc.vector.tensor_tensor(checks[:, 4:5], bounds[:, 0:1], bounds[:, 1:2], ALU.add))
            after.link(nc.vector.tensor_scalar(checks[:, 4:5], checks[:, 4:5], SPREAD, None, ALU.is_gt))
            after.link(nc.vector.tensor_tensor(checks[:, 5:6], checks[:, 2:3], checks[:, 3:4], ALU.max))
            nc.vector.tensor_tensor(checks[:, 0:1], checks[:, 5:6], checks[:, 4:5], ALU.max).then_inc(checks_ready, 1)
            dve.wait_ge(flag_ready, 1)
            needed = dve.value_load(flag[0:1, 0:1], min_val=0, max_val=1)
            with dve.If(needed != 0):
                general_vector(dve)
            dve.nop()


PACK_LINKS = 1 + (SLOTS // 8) + (SLOTS // 8 - 1) + GROUP_COLS + 1
LOGITS_LINKS = 4
FINISH_LINKS = 1
GENERAL_LINKS = 11


def diagonal(flat, start, step):
    ap = flat[:, start:start + BITS].rearrange("p (o t) -> p o t", o=1)
    dims = [list(d) for d in ap.ap]
    return bass.AP(tensor=ap.tensor, offset=ap.offset, ap=[dims[0], [step, PAIRS], [1, BITS]])


_INS = ["x", "adj", "L0_gnn_W1", "L0_gnn_b1", "L0_gnn_a1", "L0_gnn_a2", "L0_gnn_b2"]


def kernel(**inputs):
    import concourse.bacc as _bacc
    from concourse.bass_utils import run_bass_kernel_spmd as _run

    nc = _bacc.Bacc("TRN2", target_bir_lowering=False, num_devices=1)
    arrays, args = {}, []
    for name in _INS:
        a = np.ascontiguousarray(inputs[name])
        if a.ndim == 0:
            a = a.reshape(1, 1)
        arrays[name] = a
        args.append(nc.dram_tensor(name, a.shape, mybir.dt.from_np(a.dtype), kind="ExternalInput").ap())
    out = nc.dram_tensor("out", (N, D), F32, kind="ExternalOutput").ap()
    gat_kernel(nc, *args, out)
    return _run(nc, [arrays], core_ids=[0]).results[0]["out"]
```
